# Optimizing a Trainium2 kernel written in Bass

```python
import numpy as np
import jax
import jax.numpy as jnp

def _softmax(x, axis=-1):
    return jax.nn.softmax(x, axis=axis)

def _gelu(x):
    return jax.nn.gelu(x, approximate=True)

def _silu(x):
    return jax.nn.silu(x)

def _sigmoid(x):
    return jax.nn.sigmoid(x)

def _layernorm(x, axis=-1, eps=1e-05):
    m = jnp.mean(x, axis=axis, keepdims=True)
    v = jnp.var(x, axis=axis, keepdims=True)
    return (x - m) / jnp.sqrt(v + eps)

def _scatter_add(tgt, idx, src, axis=0):
    return tgt.at[idx].add(src)

def _segment_sum(src, seg, n):
    return jax.ops.segment_sum(src, seg, n)
kernel_name = 'mk_dlrm_tower_d1_rec_r8_035604'

def setup_inputs(seed: int=0):
    np.random.seed(seed)
    _w = jnp.asarray

    def _rec_inputs():
        import jax
        import jax.numpy as jnp
        _tk = jax.random.key(seed)
        dense_ctx = jax.random.normal(jax.random.fold_in(_tk, 190), (2048, 16), jnp.float32)
        ids = jnp.stack([jax.random.randint(jax.random.fold_in(_tk, 200 + f), (2048,), 0, v, jnp.int32) for f, v in enumerate([1250, 1250, 1250, 1250, 1250, 1000, 1250, 1000, 125000, 1250, 1250, 1250, 125000, 1250, 125000, 1250, 1000, 12500, 125000, 12500, 125000, 12500, 125000, 1000, 1000, 12500, 1000, 1250, 125000, 125000, 125000, 1250, 1000, 1250, 12500, 1250, 125000, 1000, 1250])], axis=1)
        tbl_0 = 0.05 * jax.random.normal(jax.random.fold_in(_tk, 500 + 0), (1250, 16), jnp.float32)
        tbl_1 = 0.05 * jax.random.normal(jax.random.fold_in(_tk, 500 + 1), (1250, 16), jnp.float32)
        tbl_2 = 0.05 * jax.random.normal(jax.random.fold_in(_tk, 500 + 2), (1250, 16), jnp.float32)
        tbl_3 = 0.05 * jax.random.normal(jax.random.fold_in(_tk, 500 + 3), (1250, 16), jnp.float32)
        tbl_4 = 0.05 * jax.random.normal(jax.random.fold_in(_tk, 500 + 4), (1250, 16), jnp.float32)
        tbl_5 = 0.05 * jax.random.normal(jax.random.fold_in(_tk, 500 + 5), (1000, 16), jnp.float32)
        tbl_6 = 0.05 * jax.random.normal(jax.random.fold_in(_tk, 500 + 6), (1250, 16), jnp.float32)
        tbl_7 = 0.05 * jax.random.normal(jax.random.fold_in(_tk, 500 + 7), (1000, 16), jnp.float32)
        tbl_8 = 0.05 * jax.random.normal(jax.random.fold_in(_tk, 500 + 8), (125000, 16), jnp.float32)
        tbl_9 = 0.05 * jax.random.normal(jax.random.fold_in(_tk, 500 + 9), (1250, 16), jnp.float32)
        tbl_10 = 0.05 * jax.random.normal(jax.random.fold_in(_tk, 500 + 10), (1250, 16), jnp.float32)
        tbl_11 = 0.05 * jax.random.normal(jax.random.fold_in(_tk, 500 + 11), (1250, 16), jnp.float32)
        tbl_12 = 0.05 * jax.random.normal(jax.random.fold_in(_tk, 500 + 12), (125000, 16), jnp.float32)
        tbl_13 = 0.05 * jax.random.normal(jax.random.fold_in(_tk, 500 + 13), (1250, 16), jnp.float32)
        tbl_14 = 0.05 * jax.random.normal(jax.random.fold_in(_tk, 500 + 14), (125000, 16), jnp.float32)
        tbl_15 = 0.05 * jax.random.normal(jax.random.fold_in(_tk, 500 + 15), (1250, 16), jnp.float32)
        tbl_16 = 0.05 * jax.random.normal(jax.random.fold_in(_tk, 500 + 16), (1000, 16), jnp.float32)
        tbl_17 = 0.05 * jax.random.normal(jax.random.fold_in(_tk, 500 + 17), (12500, 16), jnp.float32)
        tbl_18 = 0.05 * jax.random.normal(jax.random.fold_in(_tk, 500 + 18), (125000, 16), jnp.float32)
        tbl_19 = 0.05 * jax.random.normal(jax.random.fold_in(_tk, 500 + 19), (12500, 16), jnp.float32)
        tbl_20 = 0.05 * jax.random.normal(jax.random.fold_in(_tk, 500 + 20), (125000, 16), jnp.float32)
        tbl_21 = 0.05 * jax.random.normal(jax.random.fold_in(_tk, 500 + 21), (12500, 16), jnp.float32)
        tbl_22 = 0.05 * jax.random.normal(jax.random.fold_in(_tk, 500 + 22), (125000, 16), jnp.float32)
        tbl_23 = 0.05 * jax.random.normal(jax.random.fold_in(_tk, 500 + 23), (1000, 16), jnp.float32)
        tbl_24 = 0.05 * jax.random.normal(jax.random.fold_in(_tk, 500 + 24), (1000, 16), jnp.float32)
        tbl_25 = 0.05 * jax.random.normal(jax.random.fold_in(_tk, 500 + 25), (12500, 16), jnp.float32)
        tbl_26 = 0.05 * jax.random.normal(jax.random.fold_in(_tk, 500 + 26), (1000, 16), jnp.float32)
        tbl_27 = 0.05 * jax.random.normal(jax.random.fold_in(_tk, 500 + 27), (1250, 16), jnp.float32)
        tbl_28 = 0.05 * jax.random.normal(jax.random.fold_in(_tk, 500 + 28), (125000, 16), jnp.float32)
        tbl_29 = 0.05 * jax.random.normal(jax.random.fold_in(_tk, 500 + 29), (125000, 16), jnp.float32)
        tbl_30 = 0.05 * jax.random.normal(jax.random.fold_in(_tk, 500 + 30), (125000, 16), jnp.float32)
        tbl_31 = 0.05 * jax.random.normal(jax.random.fold_in(_tk, 500 + 31), (1250, 16), jnp.float32)
        tbl_32 = 0.05 * jax.random.normal(jax.random.fold_in(_tk, 500 + 32), (1000, 16), jnp.float32)
        tbl_33 = 0.05 * jax.random.normal(jax.random.fold_in(_tk, 500 + 33), (1250, 16), jnp.float32)
        tbl_34 = 0.05 * jax.random.normal(jax.random.fold_in(_tk, 500 + 34), (12500, 16), jnp.float32)
        tbl_35 = 0.05 * jax.random.normal(jax.random.fold_in(_tk, 500 + 35), (1250, 16), jnp.float32)
        tbl_36 = 0.05 * jax.random.normal(jax.random.fold_in(_tk, 500 + 36), (125000, 16), jnp.float32)
        tbl_37 = 0.05 * jax.random.normal(jax.random.fold_in(_tk, 500 + 37), (1000, 16), jnp.float32)
        tbl_38 = 0.05 * jax.random.normal(jax.random.fold_in(_tk, 500 + 38), (1250, 16), jnp.float32)
        _rk = jax.random.fold_in(_tk, 7)
        W_top1 = 0.0693375 * jax.random.normal(jax.random.fold_in(_tk, 801), (208, 512), jnp.float32)
        W_top2 = 0.0441942 * jax.random.normal(jax.random.fold_in(_tk, 802), (512, 256), jnp.float32)
        W_top3 = 0.0625 * jax.random.normal(jax.random.fold_in(_tk, 803), (256, 1), jnp.float32)
        b_top1 = jnp.zeros((512,), jnp.float32)
        b_top2 = jnp.zeros((256,), jnp.float32)
        return (dense_ctx, ids, tbl_0, tbl_1, tbl_2, tbl_3, tbl_4, tbl_5, tbl_6, tbl_7, tbl_8, tbl_9, tbl_10, tbl_11, tbl_12, tbl_13, tbl_14, tbl_15, tbl_16, tbl_17, tbl_18, tbl_19, tbl_20, tbl_21, tbl_22, tbl_23, tbl_24, tbl_25, tbl_26, tbl_27, tbl_28, tbl_29, tbl_30, tbl_31, tbl_32, tbl_33, tbl_34, tbl_35, tbl_36, tbl_37, tbl_38, W_top1, b_top1, W_top2, b_top2, W_top3)
    dense_ctx, ids, tbl_0, tbl_1, tbl_2, tbl_3, tbl_4, tbl_5, tbl_6, tbl_7, tbl_8, tbl_9, tbl_10, tbl_11, tbl_12, tbl_13, tbl_14, tbl_15, tbl_16, tbl_17, tbl_18, tbl_19, tbl_20, tbl_21, tbl_22, tbl_23, tbl_24, tbl_25, tbl_26, tbl_27, tbl_28, tbl_29, tbl_30, tbl_31, tbl_32, tbl_33, tbl_34, tbl_35, tbl_36, tbl_37, tbl_38, W_top1, b_top1, W_top2, b_top2, W_top3 = _rec_inputs()

    def _L0_rec_setup():
        import jax, jax.numpy as jnp
        import numpy as np
        key = jax.random.key(seed)
        k1, k2, k3 = jax.random.split(key, 3)
        B, F0, D = (1024, 39, 16)
        L = 128
        hash_x = jax.random.normal(k1, (B, F0, D), dtype=jnp.float32)
        W0 = jax.random.normal(k2, (F0 * F0, L), dtype=jnp.float32) * 0.05
        W1 = jax.random.normal(k3, (F0 * (L // 2), L), dtype=jnp.float32) * 0.05
        return {'hash_x': hash_x, 'W0': W0, 'W1': W1}
    _L0_rec_all = _L0_rec_setup()
    _L0_rec_in = {k: v for k, v in _L0_rec_all.items() if k in ('W0', 'W1')}
    del _L0_rec_all
    return {'dense_ctx': dense_ctx, 'ids': ids, 'tbl_0': tbl_0, 'tbl_1': tbl_1, 'tbl_2': tbl_2, 'tbl_3': tbl_3, 'tbl_4': tbl_4, 'tbl_5': tbl_5, 'tbl_6': tbl_6, 'tbl_7': tbl_7, 'tbl_8': tbl_8, 'tbl_9': tbl_9, 'tbl_10': tbl_10, 'tbl_11': tbl_11, 'tbl_12': tbl_12, 'tbl_13': tbl_13, 'tbl_14': tbl_14, 'tbl_15': tbl_15, 'tbl_16': tbl_16, 'tbl_17': tbl_17, 'tbl_18': tbl_18, 'tbl_19': tbl_19, 'tbl_20': tbl_20, 'tbl_21': tbl_21, 'tbl_22': tbl_22, 'tbl_23': tbl_23, 'tbl_24': tbl_24, 'tbl_25': tbl_25, 'tbl_26': tbl_26, 'tbl_27': tbl_27, 'tbl_28': tbl_28, 'tbl_29': tbl_29, 'tbl_30': tbl_30, 'tbl_31': tbl_31, 'tbl_32': tbl_32, 'tbl_33': tbl_33, 'tbl_34': tbl_34, 'tbl_35': tbl_35, 'tbl_36': tbl_36, 'tbl_37': tbl_37, 'tbl_38': tbl_38, 'W_top1': W_top1, 'b_top1': b_top1, 'W_top2': W_top2, 'b_top2': b_top2, 'W_top3': W_top3, 'L0_rec_W0': _L0_rec_in['W0'], 'L0_rec_W1': _L0_rec_in['W1']}

def reference(dense_ctx, ids, tbl_0, tbl_1, tbl_2, tbl_3, tbl_4, tbl_5, tbl_6, tbl_7, tbl_8, tbl_9, tbl_10, tbl_11, tbl_12, tbl_13, tbl_14, tbl_15, tbl_16, tbl_17, tbl_18, tbl_19, tbl_20, tbl_21, tbl_22, tbl_23, tbl_24, tbl_25, tbl_26, tbl_27, tbl_28, tbl_29, tbl_30, tbl_31, tbl_32, tbl_33, tbl_34, tbl_35, tbl_36, tbl_37, tbl_38, W_top1, b_top1, W_top2, b_top2, W_top3, L0_rec_W0, L0_rec_W1):
    import jax
    import jax.numpy as jnp

    def _L0_rec_ref(hash_x, W0, W1):
        import jax, jax.numpy as jnp
        import numpy as np
        x0 = hash_x
        B, F0, D = x0.shape
        L = W0.shape[1]
        z0 = jnp.einsum('bid,bjd->bdij', x0, x0).reshape(B, D, F0 * F0)
        cur0 = jax.nn.relu(jnp.einsum('bdk,kl->bld', z0, W0))
        next_h, direct0 = jnp.split(cur0, 2, axis=1)
        Fk = next_h.shape[1]
        z1 = jnp.einsum('bid,bjd->bdij', x0, next_h).reshape(B, D, F0 * Fk)
        cur1 = jax.nn.relu(jnp.einsum('bdk,kl->bld', z1, W1))
        result = jnp.concatenate([direct0, cur1], axis=1)
        return jnp.sum(result, axis=-1)
    e = jnp.stack([tbl_0[ids[:, 0]], tbl_1[ids[:, 1]], tbl_2[ids[:, 2]], tbl_3[ids[:, 3]], tbl_4[ids[:, 4]], tbl_5[ids[:, 5]], tbl_6[ids[:, 6]], tbl_7[ids[:, 7]], tbl_8[ids[:, 8]], tbl_9[ids[:, 9]], tbl_10[ids[:, 10]], tbl_11[ids[:, 11]], tbl_12[ids[:, 12]], tbl_13[ids[:, 13]], tbl_14[ids[:, 14]], tbl_15[ids[:, 15]], tbl_16[ids[:, 16]], tbl_17[ids[:, 17]], tbl_18[ids[:, 18]], tbl_19[ids[:, 19]], tbl_20[ids[:, 20]], tbl_21[ids[:, 21]], tbl_22[ids[:, 22]], tbl_23[ids[:, 23]], tbl_24[ids[:, 24]], tbl_25[ids[:, 25]], tbl_26[ids[:, 26]], tbl_27[ids[:, 27]], tbl_28[ids[:, 28]], tbl_29[ids[:, 29]], tbl_30[ids[:, 30]], tbl_31[ids[:, 31]], tbl_32[ids[:, 32]], tbl_33[ids[:, 33]], tbl_34[ids[:, 34]], tbl_35[ids[:, 35]], tbl_36[ids[:, 36]], tbl_37[ids[:, 37]], tbl_38[ids[:, 38]]], axis=1)
    z = _L0_rec_ref(e, L0_rec_W0, L0_rec_W1)
    z = z.reshape(z.shape[0], -1)
    h = jnp.concatenate([z, dense_ctx], axis=1)
    h = jnp.maximum(h @ W_top1 + b_top1, 0.0)
    h = jnp.maximum(h @ W_top2 + b_top2, 0.0)
    y = h @ W_top3
    return y

_drawn_inputs = setup_inputs


def setup_inputs(seed=0):
    import zlib

    import numpy as np

    out = dict(_drawn_inputs(seed))
    spreads = {'b_top1': (0.0, 0.8), 'b_top2': (0.0, 0.449)}
    factors = {'tbl_0': 8.0,
     'tbl_1': 8.0,
     'tbl_2': 8.0,
     'tbl_3': 8.0,
     'tbl_4': 8.0,
     'tbl_5': 8.0,
     'tbl_6': 8.0,
     'tbl_7': 8.0,
     'tbl_8': 8.0,
     'tbl_9': 8.0,
     'tbl_10': 8.0,
     'tbl_11': 8.0,
     'tbl_12': 8.0,
     'tbl_13': 8.0,
     'tbl_14': 8.0,
     'tbl_15': 8.0,
     'tbl_16': 8.0,
     'tbl_17': 8.0,
     'tbl_18': 8.0,
     'tbl_19': 8.0,
     'tbl_20': 8.0,
     'tbl_21': 8.0,
     'tbl_22': 8.0,
     'tbl_23': 8.0,
     'tbl_24': 8.0,
     'tbl_25': 8.0,
     'tbl_26': 8.0,
     'tbl_27': 8.0,
     'tbl_28': 8.0,
     'tbl_29': 8.0,
     'tbl_30': 8.0,
     'tbl_31': 8.0,
     'tbl_32': 8.0,
     'tbl_33': 8.0,
     'tbl_34': 8.0,
     'tbl_35': 8.0,
     'tbl_36': 8.0,
     'tbl_37': 8.0,
     'tbl_38': 8.0,
     'L0_rec_W1': 8.0}
    for name, (base, spread) in spreads.items():
        noise = np.random.default_rng([zlib.crc32(name.encode()), seed]).standard_normal(out[name].shape)
        drawn = base * np.exp(spread * noise) if base else spread * noise
        out[name] = jnp.asarray(drawn.astype(out[name].dtype))
    for name, factor in factors.items():
        out[name] = (out[name] * factor).astype(out[name].dtype)
    return out
```

```python
from contextlib import ExitStack

import numpy as np
import concourse.bass as bass
from concourse import mybir

B, F, D = 2048, 39, 16
L, H = 128, 64
DENSE = 16
M1, M2 = 512, 256
TILE = 128
TILES = B // TILE
DQ = 4
CHUNK = DQ * TILE
Q = D // DQ
GF = 10
FP = 4 * GF
R0 = 3
ROWS0 = R0 * F
PAIRS0 = [(b, v) for b in range(4) for v in range(2) if 6 * b + 3 * v < (F + 1) // 2]
rows0 = lambda b, v: min(R0, (F + 1) // 2 - 6 * b - 3 * v) * F
A1, J1, T1, V1 = 8, 16, 5, 4
rows1 = lambda t: min(A1, -(-(F - t) // T1)) * J1
N0, N1 = len(PAIRS0), T1 * V1


def part_row(p, f):
    return 32 * (f // GF) + GF * p + f % GF


GROUPS = [("B", b, [v for bb, v in PAIRS0 if bb == b]) for b in range(4)] + [("O", t, list(range(V1))) for t in range(T1)]
LAST_GROUPS = GROUPS[4:]
FIRST_O, LAST_B = 4, 3
COPIES = [("xs", 0, 4), ("a", 0, 5), ("v", 0, 5), ("a", 1, 6), ("v", 1, 6), ("v", 2, 7), ("v", 3, 8)]
LAST_COPIES = [c for c in COPIES if c[0] == "v"]
NG, NC = len(GROUPS), len(COPIES)
G_FIRST, C_FIRST = 4, 3 + NC


def group_at(i, q, j):
    return i * (NG * Q) + (G_FIRST + NG * q + j)


def copy_at(i, q, k):
    return i * (NC * Q) + (C_FIRST + NC * q + k)


def build(nc, ids, tables, sel_x, sel_h, w0a, w0b, w1, dense_t, wt1a, wt1b, wt2, wt3, b1, b2, out):
    f32, f32r, bf16, i32 = mybir.dt.float32, mybir.dt.float32r, mybir.dt.bfloat16, mybir.dt.int32
    ALU, ACT = mybir.AluOpType, mybir.ActivationFunctionType
    ctx = ExitStack()
    with ctx:
        sb = lambda name, shape, dt: ctx.enter_context(nc.sbuf_tensor(name, shape, dt))
        sem = lambda name: ctx.enter_context(nc.semaphore(name))
        selx = sb("selx", [128, sel_x.shape[1]], bf16)
        selh0 = sb("selh0", [128, V1 * 128], f32)
        selh = sb("selh", [128, V1 * 128], f32r)
        w0 = sb("w0", [ROWS0, N0, L], f32)
        w0t = sb("w0t", [ROWS0, N0, L], f32)
        w1s = sb("w1s", [128, N1, L], f32)
        wt1a_s = sb("wt1a_s", [H + DENSE, M1], f32)
        wt1b_s = sb("wt1b_s", [L, M1], f32)
        wt2_s = sb("wt2_s", [128, M1 // 128, M2], f32)
        wt3_s = sb("wt3_s", [128, M2 // 128], f32)
        b1_s = sb("b1_s", [128, M1 // 128], f32)
        b2_s = sb("b2_s", [128, M2 // 128], f32)
        ids_s = sb("ids_s", [128, F], i32)
        emb = sb("emb", [128, FP, D], f32)
        rest = sb("rest", [128, FP, D], f32)
        parts = sb("parts", [128, D, 128], bf16)
        xs = sb("xs", [128, Q, CHUNK], bf16)
        aa = sb("aa", [ROWS0, 2, CHUNK], f32)
        hh = sb("hh", [128, CHUNK], f32r)
        vv = sb("vv", [128, 2, V1, CHUNK], f32)
        zz = sb("zz", [128, 3, V1, CHUNK], f32)
        sum0 = sb("sum0", [128, CHUNK], f32)
        sum1 = sb("sum1", [128, CHUNK], f32)
        half0 = sb("half0", [128, CHUNK // 2], f32)
        half1 = sb("half1", [128, CHUNK // 2], f32)
        feat0 = sb("feat0", [H + DENSE, B], f32)
        feat1 = sb("feat1", [L, B], f32)
        m1 = sb("m1", [128, M1 // 128, 512], f32)
        m2 = sb("m2", [128, M2 // 128, 512], f32)
        ys = sb("ys", [1, B], f32)

        ps = lambda name: ctx.enter_context(nc.psum_tensor(name, [128, 512], f32))
        spread = [ps(f"spread{k}") for k in range(3)]
        copied = [ps(f"copied{k}") for k in range(2)]
        cur0, cur1, mlp = ps("cur0"), ps("cur1"), ps("mlp")

        consts_in = sem("consts_in")
        w1_in = sem("w1_in")
        mlp_in = sem("mlp_in")
        ids_in = sem("ids_in")
        gathers_begun = sem("gathers_begun")
        rows_in = sem("rows_in")
        zeroed = sem("zeroed")
        weights_ready = sem("weights_ready")
        high_split = sem("high_split")
        low_split = sem("low_split")
        copies_made, copies_taken = sem("copies_made"), sem("copies_taken")
        spreads_made, products_made = sem("spreads_made"), sem("products_made")
        groups_done = sem("groups_done")
        h_high, h_ready = sem("h_high"), sem("h_ready")
        sums_made = sem("sums_made")
        folds_made = sem("folds_made")
        m1_done, m1_relu, m2_done, m2_relu, y_done, y_taken = (
            sem(n) for n in ("m1_done", "m1_relu", "m2_done", "m2_relu", "y_done", "y_taken"))
        out_sent = sem("out_sent")
        CONSTS, MLPS = 4, 7

        SELA, SELB = 0, 2 * ROWS0
        SELO = SELB + 4 * ROWS0
        SELI = SELO + T1 * 128
        as_bf16 = lambda bank: bank[:, :].bitcast(bf16)
        by_field = lambda x: x[:, :, :].rearrange("s (g r) d -> s g r d", g=4)
        mlp_banks = [*spread, copied[0], copied[1], cur1]

        def part(p):
            return parts[:, :, :].rearrange("s d (g r) -> s g r d", g=4)[:, :, GF * p:GF * p + GF, :]

        with nc.Block() as block:

            @block.sync
            def _(sp):
                sp.dma_start(ids_s[:, :], ids[0:TILE, :]).then_inc(ids_in, 16)
                sp.dma_start(w0[:, :, :], w0a).then_inc(consts_in, 16)
                sp.dma_start(w0t[:, :, :], w0b).then_inc(consts_in, 16)
                sp.dma_start(selx[:, :], sel_x).then_inc(consts_in, 16)
                sp.dma_start(selh0[:, :], sel_h).then_inc(consts_in, 16)
                sp.dma_start(w1s[:, :, :], w1).then_inc(w1_in, 16)
                sp.dma_start(feat0[H:H + DENSE, :], dense_t).then_inc(mlp_in, 16)
                sp.dma_start(wt1a_s[:, :], wt1a).then_inc(mlp_in, 16)
                sp.dma_start(wt1b_s[:, :], wt1b).then_inc(mlp_in, 16)
                sp.dma_start(wt2_s[:, :, :], wt2).then_inc(mlp_in, 16)
                sp.dma_start(wt3_s[:, :], wt3).then_inc(mlp_in, 16)
                sp.dma_start(b1_s[:, :], b1).then_inc(mlp_in, 16)
                sp.dma_start(b2_s[:, :], b2).then_inc(mlp_in, 16)
                with sp.Fori(0, TILES - 1) as i:
                    sp.wait_ge(rows_in, i * (16 * F) + 16 * F)
                    sp.dma_start(ids_s[:, :], ids[bass.ds(i * TILE + TILE, TILE), :]).then_inc(ids_in, 16)
                sp.wait_ge(y_taken, B // 512 + 1)
                sp.dma_start(out, ys[:, :]).then_inc(out_sent, 16)
                sp.wait_ge(out_sent, 16)

            @block.gpsimd
            def _(pool):
                nc.gpsimd.memset(emb[:, F:FP, :], 0.0).then_inc(folds_made, 1)
                nc.gpsimd.memset(parts[:, :, :], 0.0).then_inc(zeroed, 1)

                def gather(t):
                    pool.wait_ge(ids_in, t * 16 + 16)
                    pool.sem_inc(gathers_begun, 1)
                    for f in range(F):
                        nc.gpsimd.indirect_dma_start(
                            emb[:, f, :], None, tables[f],
                            bass.IndirectOffsetOnAxis(ap=ids_s[:, f:f + 1], axis=0)).then_inc(rows_in, 16)

                def split_rests(t):
                    pool.wait_ge(high_split, t * 2 + 1)
                    nc.gpsimd.tensor_tensor(by_field(rest), by_field(emb), part(0), ALU.subtract).then_inc(low_split, 1)
                    pool.wait_ge(high_split, t * 2 + 2)
                    nc.gpsimd.tensor_tensor(part(2), by_field(rest), part(1), ALU.subtract).then_inc(low_split, 1)

                def fold(t, sums, half, feat, p0, p1, ready, done):
                    pool.wait_ge(sums_made, ready)
                    pool.wait_ge(folds_made, done - 2)
                    nc.gpsimd.tensor_tensor(half[p0:p1, :], sums[p0:p1, 0:CHUNK // 2], sums[p0:p1, CHUNK // 2:CHUNK],
                                            ALU.add).then_inc(folds_made, 1)
                    pool.wait_ge(folds_made, done - 1)
                    nc.gpsimd.tensor_tensor(feat[0:p1 - p0, bass.ds(t * TILE, TILE)], half[p0:p1, 0:TILE],
                                            half[p0:p1, TILE:2 * TILE], ALU.add).then_inc(folds_made, 1)

                def folds(t):
                    fold(t, sum0, half0, feat0, H, 2 * H, t * 8 + 7, t * 4 + 3)
                    fold(t, sum1, half1, feat1, 0, L, t * 8 + 10, t * 4 + 5)

                gather(0)
                split_rests(0)
                with pool.Fori(0, TILES - 1) as i:
                    pool.wait_ge(low_split, i * 2 + 2)
                    gather(i + 1)
                    split_rests(i + 1)
                    folds(i)
                folds(TILES - 1)

            @block.scalar
            def _(act):
                def split_parts(t):
                    act.wait_ge(rows_in, t * (16 * F) + 16 * F)
                    nc.scalar.activation(part(0), by_field(emb), ACT.Copy).then_inc(high_split, 1)
                    act.wait_ge(low_split, t * 2 + 1)
                    nc.scalar.activation(part(1), by_field(rest), ACT.Copy).then_inc(high_split, 1)

                def take(kind, k, c, bank, chunk):
                    act.wait_ge(copies_made, c + 1)
                    if kind == "xs":
                        to, of = xs[:, chunk % Q, :], as_bf16(copied[bank])[:, 0:CHUNK]
                    elif kind == "a":
                        to, of = aa[:, k, :], copied[bank][0:ROWS0, :]
                    else:
                        to, of = vv[:, chunk % 2, k, :], copied[bank][:, :]
                    nc.scalar.activation(to, of, ACT.Copy).then_inc(copies_taken, 1)

                def h_rounded(n_done, chunk_count):
                    act.wait_ge(groups_done, n_done)
                    nc.scalar.activation(hh[0:H, :], cur0[0:H, :], ACT.Relu).then_inc(h_high, 1)

                def slot(i, q, last=False):
                    if last and q == Q - 1:
                        return
                    copies = LAST_COPIES if last and q == Q - 2 else COPIES
                    if q == 2 and not last:
                        act.wait_ge(copies_made, copy_at(i, 1, 0) + 1)
                        split_parts(i + 1)
                    k0 = 0
                    if copies[0][0] == "xs":
                        take("xs", 0, copy_at(i, q, 0), copy_at(0, q, 0) % 2, q + 2)
                        k0 = 1
                    act.wait_ge(copies_made, copy_at(i, q, 0))
                    h_rounded(group_at(i, q, LAST_B) + 1, None)
                    for k, (kind, v, _) in list(enumerate(copies))[k0:]:
                        if kind == "a" and v == 0:
                            act.wait_ge(products_made, group_at(i, q, LAST_B) + 1)
                        if kind == "v" and v == 0:
                            act.wait_ge(products_made, group_at(i, q, 0))
                        take(kind, v, copy_at(i, q, k), copy_at(0, q, k) % 2, q + (1 if kind == "v" else 2))

                act.wait_ge(zeroed, 1)
                split_parts(0)
                take("xs", 0, 0, 0, 0)
                take("a", 0, 1, 1, 0)
                take("a", 1, 2, 0, 0)
                take("xs", 0, 3, 1, 1)
                h_rounded(4, 0)
                act.wait_ge(products_made, 4)
                for k, (kind, v, _) in list(enumerate(COPIES))[1:]:
                    take(kind, v, 3 + k, (3 + k) % 2, 0)
                with act.Fori(0, TILES - 1) as i:
                    for q in range(Q):
                        slot(i, q)
                for q in range(Q):
                    slot(TILES - 1, q, last=True)

                act.wait_ge(mlp_in, 16 * MLPS)
                act.sem_inc(y_taken, 1)
                with act.Fori(0, B // 512) as c:
                    for m in range(M1 // 128):
                        act.wait_ge(m1_done, c * 4 + (m + 1))
                        nc.scalar.activation(m1[:, m, :], mlp_banks[m][:, :], ACT.Relu, bias=b1_s[:, m:m + 1]).then_inc(m1_relu, 1)
                    for m in range(M2 // 128):
                        act.wait_ge(m2_done, c * 2 + (m + 1))
                        nc.scalar.activation(m2[:, m, :], mlp_banks[4 + m][:, :], ACT.Relu, bias=b2_s[:, m:m + 1]).then_inc(m2_relu, 1)
                    act.wait_ge(y_done, c + 1)
                    nc.scalar.activation(ys[0:1, bass.ds(c * 512, 512)], mlp[0:1, :], ACT.Copy).then_inc(y_taken, 1)

            @block.vector
            def _(dve):
                def product(group, u, j, z, a_or_v, chunk):
                    kind, b, vs = group
                    dve.wait_ge(spreads_made, u + 1)
                    dve.wait_ge(copies_taken, a_or_v)
                    nv = len(vs)
                    if kind == "B":
                        rows = ROWS0 if nv > 1 else rows0(b, 0)
                        other = aa[0:rows, 0:nv, :]
                    else:
                        rows = rows1(b)
                        other = vv[0:rows, chunk % 2, :, :]
                    one = spread[z][0:rows, :].unsqueeze(1).to_broadcast([rows, nv, CHUNK])
                    nc.vector.tensor_tensor(zz[0:rows, z, 0:nv, :], one, other, ALU.mult).then_inc(products_made, 1)

                def h_rest(chunk_count):
                    dve.wait_ge(h_high, chunk_count)
                    nc.vector.scalar_tensor_tensor(out=hh[H:2 * H, :], in0=cur0[0:H, :], scalar=0.0, in1=hh[0:H, :].bitcast(f32),
                                                   op0=ALU.max, op1=ALU.subtract).then_inc(h_ready, 1)

                def add_up(sums, cur, p0, p1, first, free, inc):
                    if first:
                        if free is not None:
                            dve.wait_ge(folds_made, free)
                        nc.vector.tensor_scalar(sums[p0:p1, :], cur[p0:p1, :], 0.0, None, ALU.max).then_inc(sums_made, inc)
                    else:
                        nc.vector.scalar_tensor_tensor(out=sums[p0:p1, :], in0=cur[p0:p1, :], scalar=0.0, in1=sums[p0:p1, :],
                                                       op0=ALU.max, op1=ALU.add).then_inc(sums_made, inc)

                def slot_product(i, q, j, groups=GROUPS):
                    u = group_at(i, q, j)
                    dve.wait_ge(groups_done, u - 2)
                    kind = groups[j][0]
                    a_or_v = copy_at(i, q - 1, 3) + 1 if kind == "B" else copy_at(i, q - 1, NC - 1) + 1
                    if groups is LAST_GROUPS:
                        a_or_v = copy_at(i, Q - 2, len(LAST_COPIES) - 1) + 1
                    product(groups[j], u, j, (group_at(0, q, j) + 2) % 3, a_or_v, q)

                def slot(i, q, last=False):
                    groups = LAST_GROUPS if last and q == Q - 1 else GROUPS
                    for j in range(2, len(groups)):
                        slot_product(i, q, j, groups)
                        if j == FIRST_O + 1 and groups is GROUPS:
                            h_rest(i * Q + (q + 2))
                            add_up(sum0, cur0, H, 2 * H, q == Q - 1, i * 4 + 3, 1)
                    if q < Q - 1:
                        following = LAST_GROUPS if last and q == Q - 2 else GROUPS
                        slot_product(i, q + 1, 0, following)
                        slot_product(i, q + 1, 1, following)
                    elif not last:
                        slot_product(i + 1, 0, 0)
                        slot_product(i + 1, 0, 1)
                    dve.wait_ge(groups_done, group_at(i, q, len(groups) - 1) + 1)
                    add_up(sum1, cur1, 0, L, q == 0, i * 4 + 1, 2 if groups is LAST_GROUPS else 1)

                dve.wait_ge(consts_in, 16 * CONSTS)
                nc.vector.tensor_tensor(w0[:, :, :], w0[:, :, :], w0t[:, :, :], ALU.add).then_inc(weights_ready, 1)
                nc.vector.tensor_copy(selh[:, :], selh0[:, :]).then_inc(weights_ready, 1)
                for b in range(4):
                    if b >= 3:
                        dve.wait_ge(groups_done, b - 2)
                    product(GROUPS[b], b, b, (b + 2) % 3, 3, 0)
                h_rest(1)
                add_up(sum0, cur0, H, 2 * H, True, None, 2)
                slot_product(0, 0, 0)
                slot_product(0, 0, 1)
                with dve.Fori(0, TILES - 1) as i:
                    for q in range(Q):
                        slot(i, q)
                for q in range(Q):
                    slot(TILES - 1, q, last=True)

            @block.tensor
            def _(pe):
                def make_copy(kind, k, c, bank, chunk):
                    x = xs[:, chunk % Q, :]
                    if kind == "xs":
                        for d in range(DQ):
                            last = nc.tensor.transpose(as_bf16(copied[bank])[:, d * TILE:(d + 1) * TILE],
                                                       parts[:, (chunk % Q) * DQ + d, :], selx[:, SELI:SELI + 128])
                    elif kind == "a":
                        last = nc.tensor.matmul(copied[bank][0:ROWS0, :], selx[:, SELA + k * ROWS0:SELA + (k + 1) * ROWS0], x,
                                                start=True, stop=True)
                    else:
                        last = nc.tensor.matmul(copied[bank][:, :], selh[:, k * 128:(k + 1) * 128], hh[:, :], start=True, stop=True)
                    last.then_inc(copies_made, 1)

                def make_spread(group, z, chunk):
                    kind, b, _ = group
                    at, rows = (SELB + b * ROWS0, ROWS0) if kind == "B" else (SELO + b * 128, 128)
                    nc.tensor.matmul(spread[z][0:rows, :], selx[:, at:at + rows], xs[:, chunk % Q, :],
                                     start=True, stop=True).then_inc(spreads_made, 1)

                def contract(group, u, z):
                    kind, b, vs = group
                    pe.wait_ge(products_made, u + 1)
                    for v in vs:
                        if kind == "B":
                            p = PAIRS0.index((b, v))
                            last = nc.tensor.matmul(cur0[:, :], w0[0:rows0(b, v), p, :], zz[0:rows0(b, v), z, v, :],
                                                    start=p == 0, stop=p == N0 - 1)
                        else:
                            p = b * V1 + v
                            last = nc.tensor.matmul(cur1[:, :], w1s[0:rows1(b), p, :], zz[0:rows1(b), z, v, :],
                                                    start=p == 0, stop=p == N1 - 1)
                    last.then_inc(groups_done, 1)

                def slot_copy(i, q, k, kind, v):
                    c = copy_at(i, q, k)
                    pe.wait_ge(copies_taken, c - 1)
                    if kind == "xs" and q == 2:
                        pe.wait_ge(low_split, i * 2 + 4)
                    if kind == "a" and v == 0:
                        pe.wait_ge(copies_taken, copy_at(i, q, 0) + 1)
                    if kind == "v" and v == 0:
                        pe.wait_ge(h_ready, i * Q + (q + 2))
                    make_copy(kind, v, c, copy_at(0, q, k) % 2, q + 2)

                def slot_spread(i, q, j, groups=GROUPS):
                    u = group_at(i, q, j)
                    pe.wait_ge(products_made, u - 2)
                    group = groups[j]
                    make_spread(group, (group_at(0, q, j) + 2) % 3, q + 1 if group[0] == "B" else q)

                def slot(i, q, last=False):
                    groups = LAST_GROUPS if last and q == Q - 1 else GROUPS
                    copies = COPIES
                    if last and q >= Q - 2:
                        copies = LAST_COPIES if q == Q - 2 else []
                    following = LAST_GROUPS if last and q == Q - 2 else GROUPS
                    ahead = len(groups) - 2
                    for j, group in enumerate(groups):
                        if j < ahead:
                            slot_spread(i, q, j + 2, groups)
                        elif q < Q - 1:
                            slot_spread(i, q + 1, j - ahead, following)
                        elif not last:
                            slot_spread(i + 1, 0, j - ahead)
                        for k, (kind, v, before) in enumerate(copies):
                            if before == j:
                                slot_copy(i, q, k, kind, v)
                        if group == GROUPS[0]:
                            pe.wait_ge(sums_made, i * 8 + (2 * q + 1))
                        if group == GROUPS[FIRST_O]:
                            pe.wait_ge(sums_made, i * 8 + (2 * q + 2))
                        contract(group, group_at(i, q, j), (group_at(0, q, j) + 2) % 3)

                pe.wait_ge(weights_ready, 2)
                pe.wait_ge(low_split, 2)
                make_copy("xs", 0, 0, 0, 0)
                pe.wait_ge(copies_taken, 1)
                make_copy("a", 0, 1, 1, 0)
                make_copy("a", 1, 2, 0, 0)
                for b in range(3):
                    make_spread(GROUPS[b], (b + 2) % 3, 0)
                pe.wait_ge(copies_taken, 2)
                make_copy("xs", 0, 3, 1, 1)
                for b in range(4):
                    contract(GROUPS[b], b, (b + 2) % 3)
                    if b == 0:
                        make_spread(GROUPS[3], 2, 0)
                for k, (kind, v, _) in list(enumerate(COPIES))[1:]:
                    pe.wait_ge(copies_taken, 3 + k - 1)
                    if kind == "v":
                        pe.wait_ge(h_ready, 1)
                    if kind == "a":
                        pe.wait_ge(copies_taken, 4)
                    make_copy(kind, v, 3 + k, (3 + k) % 2, 1)
                slot_spread(0, 0, 0)
                slot_spread(0, 0, 1)
                pe.wait_ge(w1_in, 16)
                with pe.Fori(0, TILES - 1) as i:
                    for q in range(Q):
                        slot(i, q)
                for q in range(Q):
                    slot(TILES - 1, q, last=True)

                pe.wait_ge(mlp_in, 16 * MLPS)
                pe.wait_ge(folds_made, 4 * TILES + 1)
                with pe.Fori(0, B // 512) as c:
                    for m in range(M1 // 128):
                        nc.tensor.matmul(mlp_banks[m][:, :], wt1a_s[:, m * 128:(m + 1) * 128],
                                         feat0[:, bass.ds(c * 512, 512)], start=True, stop=False)
                        nc.tensor.matmul(mlp_banks[m][:, :], wt1b_s[:, m * 128:(m + 1) * 128],
                                         feat1[:, bass.ds(c * 512, 512)], start=False, stop=True).then_inc(m1_done, 1)
                    for k in range(M1 // 128):
                        pe.wait_ge(m1_relu, c * 4 + (k + 1))
                        for m in range(M2 // 128):
                            last = nc.tensor.matmul(mlp_banks[4 + m][:, :], wt2_s[:, k, m * 128:(m + 1) * 128], m1[:, k, :],
                                                    start=k == 0, stop=k == M1 // 128 - 1)
                            if k == M1 // 128 - 1:
                                last.then_inc(m2_done, 1)
                    pe.wait_ge(y_taken, c + 1)
                    for k in range(M2 // 128):
                        pe.wait_ge(m2_relu, c * 2 + (k + 1))
                        last = nc.tensor.matmul(mlp[0:1, :], wt3_s[:, k:k + 1], m2[:, k, :], start=k == 0, stop=k == M2 // 128 - 1)
                    last.then_inc(y_done, 1)


def _indices():
    w0a = np.full((ROWS0, N0), -1)
    w0b = np.full((ROWS0, N0), -1)
    for p, (b, v) in enumerate(PAIRS0):
        for m in range(rows0(b, v)):
            r, i = divmod(m, F)
            x, y = (i - 3 * v) % F, (i + 6 * b + r) % F
            w0a[m, p] = x * F + y
            if x != y:
                w0b[m, p] = y * F + x
    w1 = np.full((128, N1), -1)
    for t in range(T1):
        for v in range(V1):
            for m in range(rows1(t)):
                a, j = divmod(m, J1)
                w1[m, t * V1 + v] = (T1 * a + t) * H + J1 * v + j
    return w0a, w0b, w1


def _selections():
    x = np.zeros((128, 2 * ROWS0 + 4 * ROWS0 + T1 * 128 + 128), np.float32)
    at = 0
    for v in range(2):
        for m in range(ROWS0):
            for p in range(3):
                x[part_row(p, (m % F - 3 * v) % F), at + m] = 1
        at += ROWS0
    for b in range(4):
        for m in range(ROWS0):
            for p in range(3):
                x[part_row(p, (m % F + 6 * b + m // F) % F), at + m] = 1
        at += ROWS0
    for t in range(T1):
        for m in range(rows1(t)):
            for p in range(3):
                x[part_row(p, T1 * (m // J1) + t), at + m] = 1
        at += 128
    x[:, at:] = np.eye(128)
    h = np.zeros((128, V1 * 128), np.float32)
    for v in range(V1):
        for m in range(128):
            h[J1 * v + m % J1, v * 128 + m] = h[H + J1 * v + m % J1, v * 128 + m] = 1
    return x, h


def kernel(**inputs):
    import ml_dtypes
    import concourse.bacc as _bacc
    from concourse.bass_utils import run_bass_kernel_spmd as _run

    get = lambda n: np.asarray(inputs[n])

    def rows(w, at):
        out = w[np.maximum(at, 0)]
        out[at < 0] = 0
        return np.ascontiguousarray(out)

    w0a, w0b, w1 = _indices()
    sel_x, sel_h = _selections()
    wt1 = get("W_top1")
    arrays = {
        "ids": get("ids"),
        **{f"tbl_{f}": get(f"tbl_{f}") for f in range(F)},
        "sel_x": sel_x.astype(ml_dtypes.bfloat16), "sel_h": sel_h,
        "w0a": rows(get("L0_rec_W0"), w0a), "w0b": rows(get("L0_rec_W0"), w0b), "w1": rows(get("L0_rec_W1"), w1),
        "dense_t": np.ascontiguousarray(get("dense_ctx").T),
        "wt1a": np.concatenate([wt1[:L - H], wt1[L - H + L:]], axis=0), "wt1b": wt1[L - H:L - H + L],
        "wt2": get("W_top2").reshape(M1 // 128, 128, M2).transpose(1, 0, 2),
        "wt3": get("W_top3").reshape(M2 // 128, 128).T,
        "b1": get("b_top1").reshape(M1 // 128, 128).T, "b2": get("b_top2").reshape(M2 // 128, 128).T,
    }
    arrays = {n: np.ascontiguousarray(a) for n, a in arrays.items()}
    nc = _bacc.Bacc("TRN2", target_bir_lowering=False, num_devices=1)
    d = {n: nc.dram_tensor(f"in_{n}", a.shape, mybir.dt.from_np(a.dtype), kind="ExternalInput").ap() for n, a in arrays.items()}
    out = nc.dram_tensor("out_y", (B, 1), mybir.dt.float32, kind="ExternalOutput").ap()
    build(nc, d["ids"], [d[f"tbl_{f}"] for f in range(F)], d["sel_x"], d["sel_h"], d["w0a"], d["w0b"], d["w1"], d["dense_t"],
          d["wt1a"], d["wt1b"], d["wt2"], d["wt3"], d["b1"], d["b2"], out.rearrange("b one -> one b"))
    r = _run(nc, [{f"in_{n}": a for n, a in arrays.items()}], core_ids=[0])
    return r.results[0]["out_y"]
```

```python
from contextlib import ExitStack

import numpy as np
import concourse.bass as bass
from concourse import mybir

B, F, D = 2048, 39, 16
L, H = 128, 64
DENSE = 16
M1, M2 = 512, 256
MLP_COLS = 512
TILE = 128
TILES = B // TILE
DQ = 4
CHUNK = DQ * TILE
Q = D // DQ
GF = 10
FP = 4 * GF
R0 = 3
ROWS0 = R0 * F
PAIRS0 = [(b, v) for b in range(4) for v in range(2) if 6 * b + 3 * v < (F + 1) // 2]
A1, J1, T1, V1 = 8, 16, 5, 4
N0 = len(PAIRS0)

WAYS0 = ["ff", "ff", "fd", "d"]
WAYS1 = ["ppfd"] * T1
GROUPS = [("B", b, w) for b, w in enumerate(WAYS0)] + [("O", t, w) for t, w in enumerate(WAYS1)]
LAST_GROUPS = GROUPS[4:]
FIRST_O, LAST_B = 4, 3
NG = len(GROUPS)
AHEAD = 4
ZRING = 6
PRING, DRING = 4, 4
COPIES = [("xs", 0, 1, 4), ("a", 0, 4, 5), ("a", 1, 4, 6), ("v", 0, 5, 7), ("v", 1, 6, 8), ("v", 2, 7, 9), ("v", 3, 8, 10)]
LAST_COPIES = [(kind, v, min(before, NG - 2), NG - 1) for kind, v, before, step in COPIES if kind == "v"]
NC = len(COPIES)
C_FIRST = 3 + NC
GATHERS = [{4: 1, 5: 1, 6: 1, 7: 1, 8: 8}, {8: 6}, {4: 1, 5: 1, 8: 7, 12: 1}, {4: 1, 5: 1, 6: 1, 8: 8}]
EARLY = sum(sum(g.values()) for g in GATHERS[1:])
SPLIT = [(4, 5), (7, 7)]
H_HIGH_AT = 6
H_AFTER = 6
SUM0_AFTER = 8
SUM1_AFTER = 5


def has(group, way):
    return way is None or ("d" in group[2] and len(group[2]) > 1 if way == "both" else way in group[2])


assert EARLY + sum(GATHERS[0].values()) == F
assert [len(w) for w in WAYS0] == [sum(b == k for b, _ in PAIRS0) for k in range(4)] and all(len(w) == V1 for w in WAYS1)
assert NG * Q % ZRING == 0 and NG * Q % AHEAD == 0 and NC * Q % 2 == 0
assert sum(has(g, "p") for g in GROUPS) * Q % PRING == 0 and sum(has(g, "d") for g in GROUPS) * Q % DRING == 0


def part_row(p, f):
    return 32 * (f // GF) + GF * p + f % GF


def rows0(b, v):
    return min(R0, (F + 1) // 2 - 6 * b - 3 * v) * F


def rows1(t):
    return min(A1, -(-(F - t) // T1)) * J1


def rows_of(group):
    kind, b, ways = group
    return rows1(b) if kind == "O" else min(rows0(b, v) for v in range(len(ways)))


def count_at(i, q, j, way=None, groups=GROUPS):
    n = lambda gs: sum(has(g, way) for g in gs)
    return i * (n(GROUPS) * Q) + (n(GROUPS[:4]) + n(GROUPS) * q + n(groups[:j]))


def copy_at(i, q, k):
    return i * (NC * Q) + (C_FIRST + NC * q + k)


def freed_at(i, q, j, way, ring, groups):
    order = GROUPS * 2 + groups[:j]
    back = [k for k, g in enumerate(reversed(order)) if has(g, way)][ring - 1]
    return count_at(i, q, j) - back


def groups_of(q, last):
    return LAST_GROUPS if last and q == Q - 1 else GROUPS


def copies_of(q, last):
    return COPIES if not last or q < Q - 2 else LAST_COPIES if q == Q - 2 else []


def run_ahead(i, q, last):
    at = [(i, q, j, groups_of(q, last)) for j in range(AHEAD, len(groups_of(q, last)))]
    if q < Q - 1:
        return at + [(i, q + 1, j, groups_of(q + 1, last)) for j in range(AHEAD)]
    return at if last else at + [(i + 1, 0, j, GROUPS) for j in range(AHEAD)]


def build(nc, ids, tables, sel_x, sel_h, w0a, w0b, w1, dense_t, wt1a, wt1b, wt2, wt3, b1, b2, out):
    f32, f32r, bf16, i32 = mybir.dt.float32, mybir.dt.float32r, mybir.dt.bfloat16, mybir.dt.int32
    ALU, ACT = mybir.AluOpType, mybir.ActivationFunctionType
    ctx = ExitStack()
    with ctx:
        sb = lambda name, shape, dt: ctx.enter_context(nc.sbuf_tensor(name, shape, dt))
        sem = lambda name: ctx.enter_context(nc.semaphore(name))
        selx = sb("selx", [128, sel_x.shape[1]], bf16)
        selh0 = sb("selh0", [128, V1 * 128], f32)
        selh = sb("selh", [128, V1 * 128], f32r)
        w0 = sb("w0", [ROWS0, N0, L], f32)
        w1s = sb("w1s", [128, T1, V1, L], f32)
        w0h, w0l = sb("w0h", [ROWS0, N0, L], f32r), sb("w0l", [ROWS0, N0, L], f32r)
        w1h, w1l = sb("w1h", [128, T1, V1, L], f32r), sb("w1l", [128, T1, V1, L], f32r)
        wt1a_s = sb("wt1a_s", [H + DENSE, M1], f32)
        wt1b_s = sb("wt1b_s", [L, M1], f32)
        wt2_s = sb("wt2_s", [128, M1 // 128, M2], f32)
        wt3_s = sb("wt3_s", [128, M2 // 128], f32)
        b1_s = sb("b1_s", [128, M1 // 128], f32)
        b2_s = sb("b2_s", [128, M2 // 128], f32)
        ids_a = sb("ids_a", [128, EARLY], i32)
        ids_b = sb("ids_b", [128, F - EARLY], i32)
        emb = sb("emb", [128, FP, D], f32)
        rest = sb("rest", [128, FP, D], f32)
        parts = sb("parts", [128, D, 128], bf16)
        xs = sb("xs", [128, Q, CHUNK], bf16)
        aa = sb("aa", [ROWS0, 2, CHUNK], f32)
        hh = sb("hh", [128, CHUNK], f32r)
        vv = sb("vv", [128, 2, V1, CHUNK], f32)
        zz = sb("zz", [128, ZRING, V1 - 1, CHUNK], f32)
        ph = sb("ph", [128, PRING, 2, CHUNK], f32r)
        pl = sb("pl", [128, PRING, 2, CHUNK], f32r)
        dh = sb("dh", [128, DRING, CHUNK], f32r)
        dl = sb("dl", [128, DRING, CHUNK], f32r)
        sum0 = sb("sum0", [H, CHUNK], f32)
        sum1 = sb("sum1", [128, CHUNK], f32)
        half0 = sb("half0", [H, CHUNK // 2], f32)
        half1 = sb("half1", [128, CHUNK // 2], f32)
        feat0 = sb("feat0", [H + DENSE, B], f32)
        feat1 = sb("feat1", [L, B], f32)
        w0t = zz[0:ROWS0, 0, :, :].rearrange("p v c -> p (v c)")[:, 0:N0 * L].rearrange("p (n l) -> p n l", l=L)
        m1, m2 = zz[:, 0:M1 // 128, 0, :], zz[:, 0:M2 // 128, 1, :]
        ys = sb("ys", [1, B], f32)

        ps = lambda name: ctx.enter_context(nc.psum_tensor(name, [128, 512], f32))
        spread = [ps(f"spread{k}") for k in range(AHEAD)]
        copied = [ps(f"copied{k}") for k in range(2)]
        cur0, cur1 = ps("cur0"), ps("cur1")
        mlp_banks = [*spread, *copied]

        consts_in, w1_in, mlp_in = sem("consts_in"), sem("w1_in"), sem("mlp_in")
        ida_in, idb_in = sem("ida_in"), sem("idb_in")
        gathers_begun = sem("gathers_begun")
        rows_a_in, rows_b_in = sem("rows_a_in"), sem("rows_b_in")
        zeroed = sem("zeroed")
        weights_ready = sem("weights_ready")
        w0_high, w0_split, w1_high, w1_split = sem("w0_high"), sem("w0_split"), sem("w1_high"), sem("w1_split")
        high_split = sem("high_split")
        low_split = sem("low_split")
        copies_made, copies_taken = sem("copies_made"), sem("copies_taken")
        spreads_made, products_made = sem("spreads_made"), sem("products_made")
        bank_read = sem("bank_read")
        high_p, high_d = sem("high_p"), sem("high_d")
        low_p, low_d = sem("low_p"), sem("low_d")
        groups_done = sem("groups_done")
        h_high, h_ready = sem("h_high"), sem("h_ready")
        sums0_made = sem("sums0_made")
        sums1_made = sem("sums1_made")
        folds_made = sem("folds_made")
        m1_done, m1_relu, m2_done, m2_relu = sem("m1_done"), sem("m1_relu"), sem("m2_done"), sem("m2_relu")
        y_done, y_taken = sem("y_done"), sem("y_taken")
        out_sent = sem("out_sent")
        CONSTS, MLPS = 4, 7

        SELA = 0
        SELB = SELA + 2 * ROWS0
        SELO = SELB + 4 * ROWS0
        SELI = SELO + T1 * 128
        as_bf16 = lambda bank: bank[:, :].bitcast(bf16)
        by_field = lambda x: x[:, :, :].rearrange("s (g r) d -> s g r d", g=4)
        z_of = lambda i, q, j: count_at(0, q, j) % ZRING
        p_of = lambda i, q, j, groups: count_at(0, q, j, "p", groups) % PRING
        d_of = lambda i, q, j, groups: count_at(0, q, j, "d", groups) % DRING
        bank_of = lambda i, q, j: count_at(0, q, j) % AHEAD

        def part(p):
            return parts[:, :, :].rearrange("s d (g r) -> s g r d", g=4)[:, :, GF * p:GF * p + GF, :]

        number = lambda b, way: sum(has(g, way) for g in GROUPS[:b])

        with nc.Block() as block:

            @block.sync
            def _(sp):
                sp.dma_start(ids_a[:, :], ids[0:TILE, 0:EARLY]).then_inc(ida_in, 16)
                sp.dma_start(ids_b[:, :], ids[0:TILE, EARLY:F]).then_inc(idb_in, 16)
                sp.dma_start(w0[:, :, :], w0a).then_inc(consts_in, 16)
                sp.dma_start(w0t, w0b).then_inc(consts_in, 16)
                sp.dma_start(selx[:, :], sel_x).then_inc(consts_in, 16)
                sp.dma_start(selh0[:, :], sel_h).then_inc(consts_in, 16)
                sp.dma_start(w1s[:, :, :, :], w1).then_inc(w1_in, 16)
                sp.dma_start(feat0[H:H + DENSE, :], dense_t).then_inc(mlp_in, 16)
                sp.dma_start(wt1a_s[:, :], wt1a).then_inc(mlp_in, 16)
                sp.dma_start(wt1b_s[:, :], wt1b).then_inc(mlp_in, 16)
                sp.dma_start(wt2_s[:, :, :], wt2).then_inc(mlp_in, 16)
                sp.dma_start(wt3_s[:, :], wt3).then_inc(mlp_in, 16)
                sp.dma_start(b1_s[:, :], b1).then_inc(mlp_in, 16)
                sp.dma_start(b2_s[:, :], b2).then_inc(mlp_in, 16)
                sp.wait_ge(rows_a_in, 16 * EARLY)
                sp.dma_start(ids_a[:, :], ids[TILE:2 * TILE, 0:EARLY]).then_inc(ida_in, 16)
                sp.wait_ge(rows_b_in, 16 * (F - EARLY))
                sp.dma_start(ids_b[:, :], ids[TILE:2 * TILE, EARLY:F]).then_inc(idb_in, 16)
                with sp.Fori(0, TILES - 1) as i:
                    sp.wait_ge(rows_a_in, i * (16 * EARLY) + 2 * 16 * EARLY)
                    sp.dma_start(ids_a[:, :], ids[bass.ds(i * TILE + 2 * TILE, TILE), 0:EARLY]).then_inc(ida_in, 16)
                    sp.wait_ge(rows_b_in, i * (16 * (F - EARLY)) + 2 * 16 * (F - EARLY))
                    sp.dma_start(ids_b[:, :], ids[bass.ds(i * TILE + 2 * TILE, TILE), EARLY:F]).then_inc(idb_in, 16)
                sp.wait_ge(idb_in, 16 * (TILES + 1))
                sp.wait_ge(rows_a_in, 16 * EARLY * (TILES + 1))
                sp.wait_ge(rows_b_in, 16 * (F - EARLY) * (TILES + 1))
                sp.wait_ge(y_taken, B // MLP_COLS + 1)
                sp.dma_start(out, ys[:, :]).then_inc(out_sent, 16)
                sp.wait_ge(out_sent, 16)

            @block.gpsimd
            def _(pool):
                def gather(t, first, end):
                    for f in range(first, end):
                        if f in (0, EARLY):
                            pool.wait_ge(idb_in if f else ida_in, t * 16 + 16)
                            pool.sem_inc(gathers_begun, 1)
                        at = ids_b[:, f - EARLY:f - EARLY + 1] if f >= EARLY else ids_a[:, f:f + 1]
                        nc.gpsimd.indirect_dma_start(emb[:, f, :], None, tables[f],
                                                     bass.IndirectOffsetOnAxis(ap=at, axis=0)).then_inc(rows_b_in if f >= EARLY else rows_a_in, 16)

                def split_rest(t, n):
                    pool.wait_ge(high_split, t * 2 + (n + 1))
                    if n == 0:
                        nc.gpsimd.tensor_tensor(by_field(rest), by_field(emb), part(0), ALU.subtract).then_inc(low_split, 1)
                    else:
                        nc.gpsimd.tensor_tensor(part(2), by_field(rest), part(1), ALU.subtract).then_inc(low_split, 1)

                def fold(t, sums, half, feat, rows, made, ready, done):
                    pool.wait_ge(made, ready)
                    nc.gpsimd.tensor_tensor(half[0:rows, :], sums[0:rows, 0:CHUNK // 2], sums[0:rows, CHUNK // 2:CHUNK],
                                            ALU.add).then_inc(folds_made, 1)
                    pool.wait_ge(folds_made, done - 1)
                    nc.gpsimd.tensor_tensor(feat[0:rows, bass.ds(t * TILE, TILE)], half[0:rows, 0:TILE],
                                            half[0:rows, TILE:2 * TILE], ALU.add).then_inc(folds_made, 1)

                def fold0(t):
                    fold(t, sum0, half0, feat0, H, sums0_made, t * 4 + 4, t * 4 + 3)

                def fold1(t):
                    fold(t, sum1, half1, feat1, L, sums1_made, t * 4 + 5, t * 4 + 5)

                def rests(i, q, j, groups):
                    group = groups[j]
                    n, rows, z, p = group[2].count("p"), rows_of(group), z_of(i, q, j), p_of(i, q, j, groups)
                    if n:
                        pool.wait_ge(high_p, count_at(i, q, j, "p", groups) + 1)
                        nc.gpsimd.tensor_tensor(pl[0:rows, p, 0:n, :], zz[0:rows, z, 0:n, :],
                                                ph[0:rows, p, 0:n, :].bitcast(f32), ALU.subtract).then_inc(low_p, 1)

                def slot(i, q, first=False, last=False):
                    f = sum(sum(g.values()) for g in (GATHERS[1:] if q == 0 else GATHERS[1:q]))
                    for n, at in enumerate(run_ahead(i, q, last)):
                        rests(*at)
                        if q == Q - 1 and n == 0:
                            fold0(i)
                        if q == 0 and n + AHEAD == SUM1_AFTER + 1 and not first:
                            fold1(i - 1)
                        more = GATHERS[q].get(n + AHEAD, 0)
                        if more and not last:
                            gather(i + (2 if q else 1), f, f + more)
                            f += more
                        for part_no in range(2):
                            if q == 1 and not last and n + AHEAD == SPLIT[part_no][0]:
                                split_rest(i + 1, part_no)

                nc.gpsimd.memset(emb[:, F:FP, :], 0.0).then_inc(folds_made, 1)
                nc.gpsimd.memset(parts[:, :, :], 0.0).then_inc(zeroed, 1)
                gather(0, 0, F)
                split_rest(0, 0)
                split_rest(0, 1)
                gather(1, 0, EARLY)
                for j in range(AHEAD):
                    rests(0, 0, j, GROUPS)
                slot(0, 0, first=True)
                with pool.Fori(0, TILES - 1) as i:
                    for q in range(1, Q):
                        slot(i, q)
                    slot(i + 1, 0)
                for q in range(1, Q):
                    slot(TILES - 1, q, last=True)
                fold1(TILES - 1)

            @block.scalar
            def _(act):
                def split_part(t, n):
                    if n:
                        act.wait_ge(low_split, t * 2 + 1)
                        nc.scalar.activation(part(1), by_field(rest), ACT.Copy).then_inc(high_split, 1)
                        return
                    act.wait_ge(rows_a_in, t * (16 * EARLY) + 16 * EARLY)
                    act.wait_ge(rows_b_in, t * (16 * (F - EARLY)) + 16 * (F - EARLY))
                    nc.scalar.activation(part(0), by_field(emb), ACT.Copy).then_inc(high_split, 1)

                def take(kind, k, c, bank, chunk):
                    act.wait_ge(copies_made, c + 1)
                    if kind == "xs":
                        to, of = xs[:, chunk % Q, :], as_bf16(copied[bank])[:, 0:CHUNK]
                    elif kind == "a":
                        to, of = aa[:, k, :], copied[bank][0:ROWS0, :]
                    else:
                        to, of = vv[:, chunk % 2, k, :], copied[bank][:, :]
                    nc.scalar.activation(to, of, ACT.Copy).then_inc(copies_taken, 1)

                def h_rounded(n_done):
                    act.wait_ge(groups_done, n_done)
                    nc.scalar.activation(hh[H:L, :], cur0[H:L, :], ACT.Relu).then_inc(h_high, 1)

                def rounded(group, u, z, p, d, bank, p_free=None, d_free=None):
                    n, rows = group[2].count("p"), rows_of(group)
                    if n or "d" in group[2]:
                        act.wait_ge(products_made, u + 1)
                    if n:
                        if p_free is not None:
                            act.wait_ge(groups_done, p_free)
                        nc.scalar.activation(ph[0:rows, p, 0:n, :], zz[0:rows, z, 0:n, :], ACT.Copy).then_inc(high_p, 1)
                    if "d" in group[2]:
                        if d_free is not None:
                            act.wait_ge(groups_done, d_free)
                        nc.scalar.activation(dh[0:rows, d, :], spread[bank][0:rows, :], ACT.Copy).then_inc(high_d, 1)

                def slot_rounded(i, q, j, groups):
                    rounded(groups[j], count_at(i, q, j), z_of(i, q, j), p_of(i, q, j, groups), d_of(i, q, j, groups), bank_of(i, q, j),
                            freed_at(i, q, j, "p", PRING, groups), freed_at(i, q, j, "d", DRING, groups))

                def slot(i, q, last=False):
                    for n, at in enumerate(run_ahead(i, q, last)):
                        if n + AHEAD == H_HIGH_AT and groups_of(q, last) is GROUPS:
                            act.wait_ge(copies_made, copy_at(i, q, 0))
                            h_rounded(count_at(i, q, LAST_B) + 1)
                        slot_rounded(*at)
                        for k, (kind, v, _, step) in enumerate(copies_of(q, last)):
                            if step != n + AHEAD:
                                continue
                            if kind == "a" and v == 0:
                                act.wait_ge(products_made, count_at(i, q, LAST_B) + 1)
                            if kind == "v" and v == 0:
                                act.wait_ge(products_made, count_at(i, q, 0))
                            take(kind, v, copy_at(i, q, k), copy_at(0, q, k) % 2, q + (1 if kind == "v" else 2))
                        for part_no in range(2):
                            if q == 1 and not last and n + AHEAD == SPLIT[part_no][1]:
                                act.wait_ge(copies_made, copy_at(i, 1, 0) + 1)
                                split_part(i + 1, part_no)

                act.wait_ge(weights_ready, 1)
                nc.scalar.activation(w0h[:, :, :], w0[:, :, :], ACT.Copy).then_inc(w0_high, 1)
                act.wait_ge(w1_in, 16)
                nc.scalar.activation(w1h[:, :, :, :], w1s[:, :, :, :], ACT.Copy).then_inc(w1_high, 1)
                act.wait_ge(zeroed, 1)
                split_part(0, 0)
                split_part(0, 1)
                take("xs", 0, 0, 0, 0)
                take("a", 0, 1, 1, 0)
                take("a", 1, 2, 0, 0)
                take("xs", 0, 3, 1, 1)
                for b in range(4):
                    rounded(GROUPS[b], b, b, number(b, "p"), number(b, "d"), b)
                h_rounded(4)
                act.wait_ge(products_made, 4)
                for k, (kind, v, _, _) in list(enumerate(COPIES))[1:]:
                    take(kind, v, 3 + k, (3 + k) % 2, 0)
                for j in range(AHEAD):
                    rounded(GROUPS[j], 4 + j, z_of(0, 0, j), p_of(0, 0, j, GROUPS), d_of(0, 0, j, GROUPS), bank_of(0, 0, j))
                slot(0, 0)
                with act.Fori(0, TILES - 1) as i:
                    for q in range(1, Q):
                        slot(i, q)
                    slot(i + 1, 0)
                for q in range(1, Q):
                    slot(TILES - 1, q, last=True)

                act.wait_ge(mlp_in, 16 * MLPS)
                act.sem_inc(y_taken, 1)
                with act.Fori(0, B // MLP_COLS) as c:
                    for m in range(M1 // 128):
                        act.wait_ge(m1_done, c * (M1 // 128) + (m + 1))
                        nc.scalar.activation(m1[:, m, :], mlp_banks[m][:, :], ACT.Relu, bias=b1_s[:, m:m + 1]).then_inc(m1_relu, 1)
                    for m in range(M2 // 128):
                        act.wait_ge(m2_done, c * (M2 // 128) + (m + 1))
                        nc.scalar.activation(m2[:, m, :], mlp_banks[4 + m][:, :], ACT.Relu, bias=b2_s[:, m:m + 1]).then_inc(m2_relu, 1)
                    act.wait_ge(y_done, c + 1)
                    nc.scalar.activation(ys[0:1, bass.ds(c * MLP_COLS, MLP_COLS)], cur0[0:1, :], ACT.Copy).then_inc(y_taken, 1)

            @block.vector
            def _(dve):
                def product(group, u, z, bank, taken, chunk, reads):
                    kind, b, ways = group
                    rows = rows_of(group)
                    dve.wait_ge(spreads_made, u + 1)
                    dve.wait_ge(copies_taken, taken)
                    other = aa[0:rows, :, :] if kind == "B" else vv[0:rows, chunk % 2, :, :]
                    n = len(ways) - ways.count("d")
                    if n:
                        one = spread[bank][0:rows, :].unsqueeze(1).to_broadcast([rows, n, CHUNK])
                        last = nc.vector.tensor_tensor(zz[0:rows, z, 0:n, :], one, other[:, 0:n, :], ALU.mult)
                    if "d" in ways:
                        if n:
                            last.then_inc(bank_read, 1)
                            dve.wait_ge(bank_read, reads)
                        last = nc.vector.tensor_tensor(spread[bank][0:rows, :], spread[bank][0:rows, :], other[:, n, :], ALU.mult)
                    last.then_inc(products_made, 1)

                def rest_of(group, number, d, bank):
                    rows = rows_of(group)
                    if "d" in group[2]:
                        dve.wait_ge(high_d, number + 1)
                        nc.vector.tensor_tensor(dl[0:rows, d, :], spread[bank][0:rows, :], dh[0:rows, d, :].bitcast(f32),
                                                ALU.subtract).then_inc(low_d, 1)

                def h_rest(number):
                    dve.wait_ge(h_high, number)
                    nc.vector.scalar_tensor_tensor(out=hh[0:H, :], in0=cur0[H:L, :], scalar=0.0, in1=hh[H:L, :].bitcast(f32),
                                                   op0=ALU.max, op1=ALU.subtract).then_inc(h_ready, 1)

                def add_up(sums, cur, rows, first, free, made):
                    if first:
                        if free is not None:
                            dve.wait_ge(folds_made, free)
                        nc.vector.tensor_scalar(sums[0:rows, :], cur[0:rows, :], 0.0, None, ALU.max).then_inc(made, 1)
                    else:
                        nc.vector.scalar_tensor_tensor(out=sums[0:rows, :], in0=cur[0:rows, :], scalar=0.0, in1=sums[0:rows, :],
                                                       op0=ALU.max, op1=ALU.add).then_inc(made, 1)

                def slot_product(i, q, j, groups):
                    free = count_at(i, q, j) - (ZRING - 1)
                    if not isinstance(free, int) or free > 0:
                        dve.wait_ge(groups_done, free)
                    if groups is LAST_GROUPS:
                        taken = copy_at(i, Q - 2, len(LAST_COPIES))
                    else:
                        taken = copy_at(i, q - 1, 3) if groups[j][0] == "B" else copy_at(i, q - 1, NC)
                    product(groups[j], count_at(i, q, j), z_of(i, q, j), bank_of(i, q, j), taken, q,
                            count_at(i, q, j, "both", groups) + 1)

                def slot_rest(i, q, j, groups):
                    rest_of(groups[j], count_at(i, q, j, "d", groups), d_of(i, q, j, groups), bank_of(i, q, j))

                def slot(i, q, first=False, last=False):
                    groups = groups_of(q, last)
                    before = (i, q, AHEAD - 1, groups)
                    for n, at in enumerate(run_ahead(i, q, last)):
                        slot_product(*at)
                        slot_rest(*before)
                        before = at
                        if n + AHEAD == H_AFTER and groups is GROUPS:
                            h_rest(i * Q + (q + 2))
                        if n + AHEAD == SUM0_AFTER and groups is GROUPS:
                            add_up(sum0, cur0, H, q == Q - 1, i * 4 + 3, sums0_made)
                        if n + AHEAD == (SUM1_AFTER if groups is GROUPS else AHEAD) and not first:
                            finish(i if q else i - 1, (q - 1) % Q, GROUPS)
                    if groups is LAST_GROUPS:
                        slot_rest(*before)
                    if groups is LAST_GROUPS:
                        finish(i, q, groups)

                def finish(i, q, groups):
                    dve.wait_ge(groups_done, count_at(i, q, len(groups) - 1) + 1)
                    add_up(sum1, cur1, L, q == 0, i * 4 + 1, sums1_made)

                dve.wait_ge(consts_in, 16 * CONSTS)
                nc.vector.tensor_tensor(w0[:, :, :], w0[:, :, :], w0t, ALU.add).then_inc(weights_ready, 1)
                nc.vector.tensor_copy(selh[:, :], selh0[:, :]).then_inc(weights_ready, 1)
                dve.wait_ge(w0_high, 1)
                nc.vector.tensor_tensor(w0l[:, :, :], w0[:, :, :], w0h[:, :, :].bitcast(f32), ALU.subtract).then_inc(w0_split, 1)
                dve.wait_ge(w1_high, 1)
                nc.vector.tensor_tensor(w1l[:, :, :, :], w1s[:, :, :, :], w1h[:, :, :, :].bitcast(f32), ALU.subtract).then_inc(w1_split, 1)
                for b in range(4):
                    product(GROUPS[b], b, b, b, 3, 0, number(b, "both") + 1)
                    rest_of(GROUPS[b], number(b, "d"), number(b, "d"), b)
                h_rest(1)
                add_up(sum0, cur0, H, True, None, sums0_made)
                dve.sem_inc(sums1_made, 1)
                for j in range(AHEAD):
                    slot_product(0, 0, j, GROUPS)
                    if j:
                        slot_rest(0, 0, j - 1, GROUPS)
                slot(0, 0, first=True)
                with dve.Fori(0, TILES - 1) as i:
                    for q in range(1, Q):
                        slot(i, q)
                    slot(i + 1, 0)
                for q in range(1, Q):
                    slot(TILES - 1, q, last=True)

            @block.tensor
            def _(pe):
                def make_copy(kind, k, bank, chunk):
                    x = xs[:, chunk % Q, :]
                    if kind == "xs":
                        for d in range(DQ):
                            last = nc.tensor.transpose(as_bf16(copied[bank])[:, d * TILE:(d + 1) * TILE],
                                                       parts[:, (chunk % Q) * DQ + d, :], selx[:, SELI:SELI + 128])
                    elif kind == "a":
                        last = nc.tensor.matmul(copied[bank][0:ROWS0, :], selx[:, SELA + k * ROWS0:SELA + (k + 1) * ROWS0], x,
                                                start=True, stop=True)
                    else:
                        last = nc.tensor.matmul(copied[bank][:, :], selh[:, k * 128:(k + 1) * 128], hh[:, :], start=True, stop=True)
                    last.then_inc(copies_made, 1)

                def make_spread(group, bank, chunk):
                    kind, b, _ = group
                    at, rows = (SELB + b * ROWS0, ROWS0) if kind == "B" else (SELO + b * 128, 128)
                    nc.tensor.matmul(spread[bank][0:rows, :], selx[:, at:at + rows], xs[:, chunk % Q, :],
                                     start=True, stop=True).then_inc(spreads_made, 1)

                def contract(group, u, z, p_at, d_at, p_before, d_before):
                    kind, b, ways = group
                    rows = rows_of(group)
                    acc = cur0 if kind == "B" else cur1
                    first = group in (GROUPS[0], GROUPS[FIRST_O])
                    final = group in (GROUPS[LAST_B], GROUPS[-1])
                    terms = []
                    for v in sorted(range(len(ways)), key=lambda v: ("fdp".index(ways[v]), v)):
                        if kind == "B":
                            k = PAIRS0.index((b, v))
                            w, wh, wl = w0[:, k, :], w0h[:, k, :], w0l[:, k, :]
                        else:
                            w, wh, wl = w1s[:, b, v, :], w1h[:, b, v, :], w1l[:, b, v, :]
                        if ways[v] == "f":
                            terms.append((w, zz[:, z, v, :], (products_made, u + 1)))
                        else:
                            if ways[v] == "d":
                                high, low, ready = dh[:, d_at, :], dl[:, d_at, :], (low_d, d_before + 1)
                            else:
                                high, low, ready = ph[:, p_at, v, :], pl[:, p_at, v, :], (low_p, p_before + 1)
                            terms += [(wh, high, ready), (wl, high, None), (wh, low, None)]
                    for n, (w, x, ready) in enumerate(terms):
                        if ready:
                            pe.wait_ge(*ready)
                        last = nc.tensor.matmul(acc[:, :], w[0:rows, :], x[0:rows, :], start=first and n == 0,
                                                stop=final and n == len(terms) - 1)
                    last.then_inc(groups_done, 1)

                def slot_copy(i, q, k, kind, v):
                    c = copy_at(i, q, k)
                    pe.wait_ge(copies_taken, c - 1)
                    if kind == "xs" and q == 2:
                        pe.wait_ge(low_split, i * 2 + 4)
                    if kind == "a" and v == 0:
                        pe.wait_ge(copies_taken, copy_at(i, q, 0) + 1)
                    if kind == "v" and v == 0:
                        pe.wait_ge(h_ready, i * Q + (q + 2))
                    make_copy(kind, v, copy_at(0, q, k) % 2, q + 2)

                def slot_spread(i, q, j, groups, used):
                    if has(used[3][used[2]], "d"):
                        pe.wait_ge(low_d, count_at(used[0], used[1], used[2], "d", used[3]) + 1)
                    else:
                        pe.wait_ge(products_made, count_at(*used[:3]) + 1)
                    make_spread(groups[j], bank_of(i, q, j), q + 1 if groups[j][0] == "B" else q)

                def slot(i, q, last=False):
                    groups = groups_of(q, last)
                    spreads = dict(enumerate(run_ahead(i, q, last)))
                    for j, group in enumerate(groups):
                        if j in spreads:
                            slot_spread(*spreads[j], (i, q, j, groups))
                        for k, (kind, v, before, _) in enumerate(copies_of(q, last)):
                            if before == j:
                                slot_copy(i, q, k, kind, v)
                        if group == GROUPS[0]:
                            pe.wait_ge(sums0_made, i * 4 + (q + 1))
                        if group == GROUPS[FIRST_O]:
                            pe.wait_ge(sums1_made, i * 4 + (q + 1))
                        contract(group, count_at(i, q, j), z_of(i, q, j), p_of(i, q, j, groups), d_of(i, q, j, groups),
                                 count_at(i, q, j, "p", groups), count_at(i, q, j, "d", groups))

                pe.wait_ge(weights_ready, 2)
                pe.wait_ge(low_split, 2)
                make_copy("xs", 0, 0, 0)
                pe.wait_ge(copies_taken, 1)
                make_copy("a", 0, 1, 0)
                make_copy("a", 1, 0, 0)
                for b in range(4):
                    make_spread(GROUPS[b], b, 0)
                pe.wait_ge(copies_taken, 2)
                make_copy("xs", 0, 1, 1)
                pe.wait_ge(w0_split, 1)
                for b in range(4):
                    contract(GROUPS[b], b, b, number(b, "p"), number(b, "d"), number(b, "p"), number(b, "d"))
                for k, (kind, v, _, _) in list(enumerate(COPIES))[1:]:
                    pe.wait_ge(copies_taken, max(C_FIRST - NC + k - 1, 4))
                    if kind == "v":
                        pe.wait_ge(h_ready, 1)
                    make_copy(kind, v, (C_FIRST - NC + k) % 2, 1)
                pe.wait_ge(products_made, 4)
                pe.wait_ge(low_d, number(4, "d"))
                for j in range(AHEAD):
                    make_spread(GROUPS[j], bank_of(0, 0, j), 1)
                pe.wait_ge(w1_split, 1)
                slot(0, 0)
                with pe.Fori(0, TILES - 1) as i:
                    for q in range(1, Q):
                        slot(i, q)
                    slot(i + 1, 0)
                for q in range(1, Q):
                    slot(TILES - 1, q, last=True)

                pe.wait_ge(mlp_in, 16 * MLPS)
                pe.wait_ge(folds_made, 4 * TILES + 1)
                with pe.Fori(0, B // MLP_COLS) as c:
                    cols = bass.ds(c * MLP_COLS, MLP_COLS)
                    for m in range(M1 // 128):
                        nc.tensor.matmul(mlp_banks[m][:, :], wt1a_s[:, m * 128:(m + 1) * 128], feat0[:, cols], start=True, stop=False)
                        nc.tensor.matmul(mlp_banks[m][:, :], wt1b_s[:, m * 128:(m + 1) * 128], feat1[:, cols],
                                         start=False, stop=True).then_inc(m1_done, 1)
                    for k in range(M1 // 128):
                        pe.wait_ge(m1_relu, c * (M1 // 128) + (k + 1))
                        for m in range(M2 // 128):
                            last = nc.tensor.matmul(mlp_banks[4 + m][:, :], wt2_s[:, k, m * 128:(m + 1) * 128], m1[:, k, :],
                                                    start=k == 0, stop=k == M1 // 128 - 1)
                            if k == M1 // 128 - 1:
                                last.then_inc(m2_done, 1)
                    pe.wait_ge(y_taken, c + 1)
                    for k in range(M2 // 128):
                        pe.wait_ge(m2_relu, c * (M2 // 128) + (k + 1))
                        last = nc.tensor.matmul(cur0[0:1, :], wt3_s[:, k:k + 1], m2[:, k, :], start=k == 0, stop=k == M2 // 128 - 1)
                    last.then_inc(y_done, 1)


def _indices():
    w0a = np.full((ROWS0, N0), -1)
    w0b = np.full((ROWS0, N0), -1)
    for p, (b, v) in enumerate(PAIRS0):
        for m in range(rows0(b, v)):
            r, i = divmod(m, F)
            x, y = (i - 3 * v) % F, (i + 6 * b + r) % F
            w0a[m, p] = x * F + y
            if x != y:
                w0b[m, p] = y * F + x
    w1 = np.full((128, T1 * V1), -1)
    for t in range(T1):
        for v in range(V1):
            for m in range(rows1(t)):
                a, j = divmod(m, J1)
                w1[m, t * V1 + v] = (T1 * a + t) * H + J1 * v + j
    return w0a, w0b, w1


def _selections():
    x = np.zeros((128, 2 * ROWS0 + 4 * ROWS0 + T1 * 128 + 128), np.float32)
    at = 0
    for v in range(2):
        for m in range(ROWS0):
            for p in range(3):
                x[part_row(p, (m % F - 3 * v) % F), at + m] = 1
        at += ROWS0
    for b in range(4):
        for m in range(ROWS0):
            for p in range(3):
                x[part_row(p, (m % F + 6 * b + m // F) % F), at + m] = 1
        at += ROWS0
    for t in range(T1):
        for m in range(rows1(t)):
            for p in range(3):
                x[part_row(p, T1 * (m // J1) + t), at + m] = 1
        at += 128
    x[:, at:] = np.eye(128)
    h = np.zeros((128, V1 * 128), np.float32)
    for v in range(V1):
        for m in range(128):
            h[J1 * v + m % J1, v * 128 + m] = h[H + J1 * v + m % J1, v * 128 + m] = 1
    return x, h


def kernel(**inputs):
    import ml_dtypes
    import concourse.bacc as _bacc
    from concourse.bass_utils import run_bass_kernel_spmd as _run

    get = lambda n: np.asarray(inputs[n])

    def rows(w, at):
        out = w[np.maximum(at, 0)]
        out[at < 0] = 0
        return np.ascontiguousarray(out)

    w0a, w0b, w1 = _indices()
    sel_x, sel_h = _selections()
    wt1 = get("W_top1")
    wl0 = np.concatenate([get("L0_rec_W0")[:, H:], get("L0_rec_W0")[:, :H]], axis=1)
    arrays = {
        "ids": np.concatenate([get("ids"), np.zeros((TILE, F), get("ids").dtype)], axis=0),
        **{f"tbl_{f}": get(f"tbl_{f}") for f in range(F)},
        "sel_x": sel_x.astype(ml_dtypes.bfloat16), "sel_h": sel_h,
        "w0a": rows(wl0, w0a), "w0b": rows(wl0, w0b), "w1": rows(get("L0_rec_W1"), w1).reshape(128, T1, V1, L),
        "dense_t": np.ascontiguousarray(get("dense_ctx").T),
        "wt1a": np.concatenate([wt1[:L - H], wt1[L - H + L:]], axis=0), "wt1b": wt1[L - H:L - H + L],
        "wt2": get("W_top2").reshape(M1 // 128, 128, M2).transpose(1, 0, 2),
        "wt3": get("W_top3").reshape(M2 // 128, 128).T,
        "b1": get("b_top1").reshape(M1 // 128, 128).T, "b2": get("b_top2").reshape(M2 // 128, 128).T,
    }
    arrays = {n: np.ascontiguousarray(a) for n, a in arrays.items()}
    nc = _bacc.Bacc("TRN2", target_bir_lowering=False, num_devices=1)
    d = {n: nc.dram_tensor(f"in_{n}", a.shape, mybir.dt.from_np(a.dtype), kind="ExternalInput").ap() for n, a in arrays.items()}
    out = nc.dram_tensor("out_y", (B, 1), mybir.dt.float32, kind="ExternalOutput").ap()
    build(nc, d["ids"], [d[f"tbl_{f}"] for f in range(F)], d["sel_x"], d["sel_h"], d["w0a"], d["w0b"], d["w1"], d["dense_t"],
          d["wt1a"], d["wt1b"], d["wt2"], d["wt3"], d["b1"], d["b2"], out.rearrange("b one -> one b"))
    r = _run(nc, [{f"in_{n}": a for n, a in arrays.items()}], core_ids=[0])
    return r.results[0]["out_y"]
```

```python
from contextlib import ExitStack

import numpy as np
import concourse.bass as bass
from concourse import mybir

B, F, D = 2048, 39, 16
L, H = 128, 64
DENSE = 16
M1, M2 = 512, 256
MLP_COLS = 512
STEPS = B // MLP_COLS
TILE = 128
TILES = B // TILE
DQ = 4
CHUNK = DQ * TILE
Q = D // DQ
GF = 10
FP = 4 * GF
R0, B0, V0 = 3, 2, 4
ROWS0 = R0 * F
PAIRS0 = [(b, v) for b in range(B0) for v in range(V0) if R0 * (V0 * b + v) < (F + 1) // 2]
ROWSA = ROWS0 + R0 * (V0 - 1)
A1, J1, T1, V1 = 8, 16, 5, 4
N0 = len(PAIRS0)

WAYS0 = ["fffd", "ffd"]
WAYS1 = ["ppfd"] * T1
GROUPS = [("B", b, w) for b, w in enumerate(WAYS0)] + [("O", t, w) for t, w in enumerate(WAYS1)]
LAST_GROUPS = GROUPS[B0:]
NG = len(GROUPS)
AHEAD = 4
ZRING = 7
PRING, DRING = 4, 4
COPIES = [("xs", 1, 4), ("a", 2, 4)]
NC = len(COPIES)
C_FIRST = 2 + NC
GATHERS = [{4: 1, 5: 1, 6: 6, 8: 5, 9: 1}, {7: 1, 8: 3, 9: 1, 10: 1}, {4: 1, 7: 3, 8: 4, 9: 3}, {5: 1, 6: 2, 7: 2, 8: 2, 10: 1}]
EARLY = sum(sum(g.values()) for g in GATHERS[1:])
SPLIT = [(6, 5), (7, 6)]
H_AT = 5
SUM0_AFTER = 5
SUM1_AFTER = 4


def has(group, way):
    return way is None or (group[2].strip("d") != "" if way == "z" else way in group[2])


assert EARLY + sum(GATHERS[0].values()) == F
assert all(AHEAD <= k < NG + AHEAD for g in GATHERS for k in g) and AHEAD < H_AT <= NG
assert [len(w) for w in WAYS0] == [sum(b == k for b, _ in PAIRS0) for k in range(B0)] and all(len(w) == V1 for w in WAYS1)
assert NG * Q % ZRING == 0 and NG * Q % AHEAD == 0 and NC * Q % 2 == 0
assert sum(has(g, "p") for g in GROUPS) * Q % PRING == 0 and sum(has(g, "d") for g in GROUPS) * Q % DRING == 0


def part_row(p, f):
    return 32 * (f // GF) + GF * p + f % GF


def rows_of(group):
    return A1 * J1 if group[0] == "O" else ROWS0


def count_at(i, q, j, way=None, groups=GROUPS):
    n = lambda gs: sum(has(g, way) for g in gs)
    return i * (n(GROUPS) * Q) + (n(GROUPS[:B0]) + n(GROUPS) * q + n(groups[:j]))


def copy_at(i, q, k):
    return i * (NC * Q) + (C_FIRST + NC * q + k)


def freed_at(i, q, j, way, ring, groups):
    order = GROUPS * 2 + groups[:j]
    back = [k for k, g in enumerate(reversed(order)) if has(g, way)][ring - 1]
    return count_at(i, q, j) - back


def groups_of(q, last):
    return LAST_GROUPS if last and q == Q - 1 else GROUPS


def copies_of(q, last):
    return COPIES if not last or q < Q - 2 else []


def run_ahead(i, q, last):
    at = [(i, q, j, groups_of(q, last)) for j in range(AHEAD, len(groups_of(q, last)))]
    if q < Q - 1:
        return at + [(i, q + 1, j, groups_of(q + 1, last)) for j in range(AHEAD)]
    return at if last else at + [(i + 1, 0, j, GROUPS) for j in range(AHEAD)]


def build(nc, ids, tables, sel_x, w0a, w0b, w1, dense_t, wts, wt3, b1, b2, out):
    f32, f32r, bf16, i32 = mybir.dt.float32, mybir.dt.float32r, mybir.dt.bfloat16, mybir.dt.int32
    ALU, ACT = mybir.AluOpType, mybir.ActivationFunctionType
    ctx = ExitStack()
    with ctx:
        sb = lambda name, shape, dt: ctx.enter_context(nc.sbuf_tensor(name, shape, dt))
        sem = lambda name: ctx.enter_context(nc.semaphore(name))
        selx = sb("selx", [128, sel_x.shape[1]], bf16)
        w0 = sb("w0", [ROWS0, N0, L], f32)
        w1s = sb("w1s", [128, T1, V1, L], f32)
        w0h, w0l = sb("w0h", [ROWS0, N0, L], f32r), sb("w0l", [ROWS0, N0, L], f32r)
        w1h, w1l = sb("w1h", [128, T1, V1, L], f32r), sb("w1l", [128, T1, V1, L], f32r)
        wth = sb("wth", [128, 2 * M1 + M1 // 128 * M2], f32r)
        wtl = sb("wtl", [128, 2 * M1 + M1 // 128 * M2], f32r)
        wt3_s = sb("wt3_s", [128, M2 // 128], f32)
        b1_s = sb("b1_s", [128, M1 // 128], f32)
        b2_s = sb("b2_s", [128, M2 // 128], f32)
        ids_a = sb("ids_a", [128, EARLY], i32)
        ids_b = sb("ids_b", [128, F - EARLY], i32)
        emb = sb("emb", [128, FP, D], f32)
        rest = sb("rest", [128, FP, D], f32)
        parts = sb("parts", [128, D, 128], bf16)
        xs = sb("xs", [128, Q, CHUNK], bf16)
        aa = sb("aa", [ROWSA, V0, CHUNK], f32)
        vv = sb("vv", [128, 2, V1, CHUNK], f32)
        zz = sb("zz", [128, ZRING, V1 - 1, CHUNK], f32)
        ph = sb("ph", [128, PRING, 2, CHUNK], f32r)
        pl = sb("pl", [128, PRING, 2, CHUNK], f32r)
        dh = sb("dh", [128, DRING, CHUNK], f32r)
        dl = sb("dl", [128, DRING, CHUNK], f32r)
        s0h = sb("s0h", [128, CHUNK], f32)
        sum0, hh = s0h[0:H, :], s0h[H:L, :]
        sum1 = sb("sum1", [128, CHUNK], f32)
        half = sb("half", [128, CHUNK // 2], f32)
        feat0 = sb("feat0", [H + DENSE, B], f32)
        feat1 = sb("feat1", [L, B], f32)
        zz_flat = zz[:, :, :, :].rearrange("p r v c -> p (r v c)")
        w0t = zz_flat[0:ROWS0, 0:N0 * L].rearrange("p (n l) -> p n l", l=L)
        wt = zz_flat[:, 3 * CHUNK:3 * CHUNK + 2 * M1 + M1 // 128 * M2]
        feat_high = ph[:, :, :, :].rearrange("p r v c -> p (r v c)")
        feat_low = pl[:, :, :, :].rearrange("p r v c -> p (r v c)")
        m1, m1_high, m1_low, m2 = zz[:, 0:M1 // 128, 0, :], dh, dl, zz[:, 0:M2 // 128, 1, :]
        ys = vv[0:1, 0, :, :].rearrange("p v c -> p (v c)")[:, 0:B]

        ps = lambda name: ctx.enter_context(nc.psum_tensor(name, [128, 512], f32))
        spread = [ps(f"spread{k}") for k in range(AHEAD)]
        copied = [ps(f"copied{k}") for k in range(2)]
        cur0, cur1 = ps("cur0"), ps("cur1")
        mlp_banks = [*spread, *copied]

        consts_in, w1_in, mlp_in = sem("consts_in"), sem("w1_in"), sem("mlp_in")
        ida_in, idb_in = sem("ida_in"), sem("idb_in")
        gathers_begun = sem("gathers_begun")
        rows_a_in, rows_b_in = sem("rows_a_in"), sem("rows_b_in")
        zeroed = sem("zeroed")
        weights_ready = sem("weights_ready")
        w0_high, w0_split, w1_high, w1_split = sem("w0_high"), sem("w0_split"), sem("w1_high"), sem("w1_split")
        high_split = sem("high_split")
        low_split = sem("low_split")
        copies_made, copies_taken = sem("copies_made"), sem("copies_taken")
        spreads_made = sem("spreads_made")
        zz_made, d_made = sem("zz_made"), sem("d_made")
        aa_laid = sem("aa_laid")
        high_p, high_d = sem("high_p"), sem("high_d")
        low_p, low_d = sem("low_p"), sem("low_d")
        groups_done = sem("groups_done")
        h_made, h_laid = sem("h_made"), sem("h_laid")
        sums0_made = sem("sums0_made")
        sums1_made = sem("sums1_made")
        folds_made = sem("folds_made")
        m1_done, m1_relu, m2_done, m2_relu = sem("m1_done"), sem("m1_relu"), sem("m2_done"), sem("m2_relu")
        y_done, y_taken = sem("y_done"), sem("y_taken")
        out_sent = sem("out_sent")
        wt_high, wt_split = sem("wt_high"), sem("wt_split")
        feat_rounded, feat_split = sem("feat_rounded"), sem("feat_split")
        m1_rounded, m1_split = sem("m1_rounded"), sem("m1_split")
        wt_in = sem("wt_in")
        CONSTS, MLPS, AA = 3, 4, 16 * (V0 - 1)

        SELA = 0
        SELB = SELA + ROWSA
        SELO = SELB + B0 * ROWS0
        SELI = SELO + T1 * 128
        as_bf16 = lambda bank: bank[:, :].bitcast(bf16)
        by_field = lambda x: x[:, :, :].rearrange("s (g r) d -> s g r d", g=4)
        z_of = lambda i, q, j: count_at(0, q, j) % ZRING
        p_of = lambda i, q, j, groups: count_at(0, q, j, "p", groups) % PRING
        d_of = lambda i, q, j, groups: count_at(0, q, j, "d", groups) % DRING
        bank_of = lambda i, q, j: count_at(0, q, j) % AHEAD

        def part(p):
            return parts[:, :, :].rearrange("s d (g r) -> s g r d", g=4)[:, :, GF * p:GF * p + GF, :]

        number = lambda b, way: sum(has(g, way) for g in GROUPS[:b])

        with nc.Block() as block:

            @block.sync
            def _(sp):
                sp.dma_start(ids_a[:, :], ids[0:TILE, 0:EARLY]).then_inc(ida_in, 16)
                sp.dma_start(ids_b[:, :], ids[0:TILE, EARLY:F]).then_inc(idb_in, 16)
                sp.dma_start(w0[:, :, :], w0a).then_inc(consts_in, 16)
                sp.dma_start(w0t, w0b).then_inc(consts_in, 16)
                sp.dma_start(selx[:, :], sel_x).then_inc(consts_in, 16)
                sp.dma_start(w1s[:, :, :, :], w1).then_inc(w1_in, 16)
                sp.dma_start(feat0[H:H + DENSE, :], dense_t).then_inc(mlp_in, 16)
                sp.dma_start(wt, wts).then_inc(wt_in, 16)
                sp.dma_start(wt3_s[:, :], wt3).then_inc(mlp_in, 16)
                sp.dma_start(b1_s[:, :], b1).then_inc(mlp_in, 16)
                sp.dma_start(b2_s[:, :], b2).then_inc(mlp_in, 16)

                def ids_a_of(t):
                    sp.wait_ge(rows_a_in, t * (16 * EARLY))
                    sp.dma_start(ids_a[:, :], ids[bass.ds(t * TILE, TILE), 0:EARLY]).then_inc(ida_in, 16)

                def ids_b_of(t):
                    sp.wait_ge(rows_b_in, t * (16 * (F - EARLY)))
                    sp.dma_start(ids_b[:, :], ids[bass.ds(t * TILE, TILE), EARLY:F]).then_inc(idb_in, 16)

                def lay_h(chunk, number):
                    sp.wait_ge(h_made, number + 1)
                    for v in range(V1):
                        rows = s0h[H + J1 * v:H + J1 * (v + 1), :].unsqueeze(1).to_broadcast([J1, A1, CHUNK])
                        sp.dma_start(vv[:, chunk % 2, v, :], rows).then_inc(h_laid, 16)

                def lay_aa(copies):
                    sp.wait_ge(copies_taken, copies)
                    for v in range(V0 - 1):
                        at = R0 * (V0 - 1 - v)
                        sp.dma_start(aa[0:ROWS0, v, :], aa[at:at + ROWS0, V0 - 1, :]).then_inc(aa_laid, 16)

                def slot(i, q, last=False):
                    if not last or q < Q - 2:
                        lay_aa(copy_at(i, q, NC))
                    if not last or q < Q - 1:
                        lay_h(q + 1, i * Q + (q + 1))
                    if q == 0:
                        ids_a_of(i + 2)
                    if q == 1 and not last:
                        ids_b_of(i + 2)

                ids_a_of(1)
                ids_b_of(1)
                lay_aa(2)
                lay_aa(C_FIRST)
                lay_h(0, 0)
                slot(0, 0)
                with sp.Fori(0, TILES - 1) as i:
                    for q in range(1, Q):
                        slot(i, q)
                    slot(i + 1, 0)
                for q in range(1, Q):
                    slot(TILES - 1, q, last=True)
                sp.wait_ge(ida_in, 16 * (TILES + 2))
                sp.wait_ge(idb_in, 16 * (TILES + 1))
                sp.wait_ge(rows_a_in, 16 * EARLY * (TILES + 1))
                sp.wait_ge(rows_b_in, 16 * (F - EARLY) * (TILES + 1))
                sp.wait_ge(y_taken, STEPS + 1)
                sp.dma_start(out, ys).then_inc(out_sent, 16)
                sp.wait_ge(out_sent, 16)

            @block.gpsimd
            def _(pool):
                def gather(t, first, end):
                    for f in range(first, end):
                        if f in (0, EARLY):
                            pool.wait_ge(idb_in if f else ida_in, t * 16 + 16)
                            if f == 0 and not (isinstance(t, int) and t == 0):
                                pool.wait_ge(low_split, t * 2 - 1)
                            pool.sem_inc(gathers_begun, 1)
                        at = ids_b[:, f - EARLY:f - EARLY + 1] if f >= EARLY else ids_a[:, f:f + 1]
                        nc.gpsimd.indirect_dma_start(
                            emb[:, f, :], None, tables[f], bass.IndirectOffsetOnAxis(ap=at, axis=0),
                        ).then_inc(rows_b_in if f >= EARLY else rows_a_in, 16)

                def rests(group, z, p, before):
                    n, rows = group[2].count("p"), rows_of(group)
                    if n:
                        pool.wait_ge(high_p, before + 1)
                        nc.gpsimd.tensor_tensor(pl[0:rows, p, 0:n, :], zz[0:rows, z, 0:n, :],
                                                ph[0:rows, p, 0:n, :].bitcast(f32), ALU.subtract).then_inc(low_p, 1)

                def slot_rests(i, q, j, groups):
                    rests(groups[j], z_of(i, q, j), p_of(i, q, j, groups), count_at(i, q, j, "p", groups))

                def slot(i, q, last=False):
                    f = sum(sum(g.values()) for g in (GATHERS[1:] if q == 0 else GATHERS[1:q]))
                    for n, at in enumerate(run_ahead(i, q, last)):
                        slot_rests(*at)
                        more = GATHERS[q].get(n + AHEAD, 0)
                        if more and not last:
                            gather(i + (2 if q else 1), f, f + more)
                            f += more

                nc.gpsimd.memset(emb[:, F:FP, :], 0.0).then_inc(zeroed, 1)
                nc.gpsimd.memset(parts[:, :, :], 0.0).then_inc(zeroed, 1)
                gather(0, 0, F)
                for b in range(B0):
                    rests(GROUPS[b], b, number(b, "p"), number(b, "p"))
                gather(1, 0, EARLY)
                for j in range(AHEAD):
                    slot_rests(0, 0, j, GROUPS)
                slot(0, 0)
                with pool.Fori(0, TILES - 1) as i:
                    for q in range(1, Q):
                        slot(i, q)
                    slot(i + 1, 0)
                for q in range(1, Q):
                    slot(TILES - 1, q, last=True)

            @block.scalar
            def _(act):
                def split_part(t, n):
                    if n:
                        act.wait_ge(low_split, t * 2 + 1)
                        nc.scalar.activation(part(1), by_field(rest), ACT.Copy).then_inc(high_split, 1)
                        return
                    act.wait_ge(rows_a_in, t * (16 * EARLY) + 16 * EARLY)
                    act.wait_ge(rows_b_in, t * (16 * (F - EARLY)) + 16 * (F - EARLY))
                    nc.scalar.activation(part(0), by_field(emb), ACT.Copy).then_inc(high_split, 1)

                def take(kind, c, bank, chunk):
                    act.wait_ge(copies_made, c + 1)
                    if kind == "xs":
                        to, of = xs[:, chunk % Q, :], as_bf16(copied[bank])[:, 0:CHUNK]
                    else:
                        to, of = aa[:, V0 - 1, :], copied[bank][0:ROWSA, :]
                    nc.scalar.activation(to, of, ACT.Copy).then_inc(copies_taken, 1)

                def make_h(n_done, laid):
                    act.wait_ge(groups_done, n_done)
                    if laid is not None:
                        act.wait_ge(h_laid, laid)
                    nc.scalar.activation(hh, cur0[H:L, :], ACT.Relu).then_inc(h_made, 1)

                def rounded(group, z, p, d, bank, z_before, d_before, p_free=None, d_free=None):
                    n, rows = group[2].count("p"), rows_of(group)
                    if n:
                        act.wait_ge(zz_made, z_before + 1)
                        if p_free is not None:
                            act.wait_ge(groups_done, p_free)
                        nc.scalar.activation(ph[0:rows, p, 0:n, :], zz[0:rows, z, 0:n, :], ACT.Copy).then_inc(high_p, 1)
                    if "d" in group[2]:
                        act.wait_ge(d_made, d_before + 1)
                        if d_free is not None:
                            act.wait_ge(groups_done, d_free)
                        nc.scalar.activation(dh[0:rows, d, :], spread[bank][0:rows, :], ACT.Copy).then_inc(high_d, 1)

                def slot_rounded(i, q, j, groups):
                    rounded(groups[j], z_of(i, q, j), p_of(i, q, j, groups), d_of(i, q, j, groups), bank_of(i, q, j),
                            count_at(i, q, j, "z", groups), count_at(i, q, j, "d", groups),
                            freed_at(i, q, j, "p", PRING, groups), freed_at(i, q, j, "d", DRING, groups))

                def slot(i, q, last=False):
                    for n, at in enumerate(run_ahead(i, q, last)):
                        if n + AHEAD == H_AT and groups_of(q, last) is GROUPS:
                            make_h(count_at(i, q, B0), i * (Q * V1 * 16) + (q + 1) * (V1 * 16))
                        slot_rounded(*at)
                        for k, (kind, _, step) in enumerate(copies_of(q, last)):
                            if step != n + AHEAD:
                                continue
                            if kind == "a":
                                act.wait_ge(zz_made, count_at(i, q, B0, "z"))
                                act.wait_ge(d_made, count_at(i, q, B0, "d"))
                            take(kind, copy_at(i, q, k), copy_at(0, q, k) % 2, q + 2)
                        for part_no in range(2):
                            if q == 1 and not last and n + AHEAD == SPLIT[part_no][1]:
                                act.wait_ge(copies_made, copy_at(i, 1, 0) + 1)
                                split_part(i + 1, part_no)

                act.wait_ge(weights_ready, 1)
                nc.scalar.activation(w0h[:, :, :], w0[:, :, :], ACT.Copy).then_inc(w0_high, 1)
                act.wait_ge(w1_in, 16)
                nc.scalar.activation(w1h[:, :, :, :], w1s[:, :, :, :], ACT.Copy).then_inc(w1_high, 1)
                act.wait_ge(wt_in, 16)
                nc.scalar.activation(wth[:, :], wt, ACT.Copy).then_inc(wt_high, 1)
                act.wait_ge(zeroed, 2)
                split_part(0, 0)
                split_part(0, 1)
                take("xs", 0, 0, 0)
                take("a", 1, 1, 0)
                take("xs", 2, 0, 1)
                for b in range(B0):
                    rounded(GROUPS[b], b, number(b, "p"), number(b, "d"), b, number(b, "z"), number(b, "d"))
                act.wait_ge(zz_made, number(B0, "z"))
                act.wait_ge(d_made, number(B0, "d"))
                take("a", 3, 1, 1)
                make_h(B0, None)
                for j in range(AHEAD):
                    rounded(GROUPS[j], z_of(0, 0, j), p_of(0, 0, j, GROUPS), d_of(0, 0, j, GROUPS), bank_of(0, 0, j),
                            count_at(0, 0, j, "z"), count_at(0, 0, j, "d"))
                slot(0, 0)
                with act.Fori(0, TILES - 1) as i:
                    for q in range(1, Q):
                        slot(i, q)
                    slot(i + 1, 0)
                for q in range(1, Q):
                    slot(TILES - 1, q, last=True)

                act.wait_ge(mlp_in, 16 * MLPS)
                act.sem_inc(y_taken, 1)
                act.wait_ge(groups_done, count_at(TILES - 1, Q - 1, len(LAST_GROUPS)))

                def features(c):
                    for n, (feat, rows) in enumerate([(feat0, H + DENSE), (feat1, L)]):
                        nc.scalar.activation(feat_high[0:rows, bass.ds(c * (2 * MLP_COLS) + n * MLP_COLS, MLP_COLS)],
                                             feat[:, bass.ds(c * MLP_COLS, MLP_COLS)], ACT.Copy).then_inc(feat_rounded, 1)

                act.wait_ge(folds_made, 4 * TILES - 3)
                with act.Fori(0, STEPS - 1) as c:
                    features(c)
                act.wait_ge(folds_made, 4 * TILES + 1)
                features(STEPS - 1)
                with act.Fori(0, STEPS) as c:
                    for m in range(M1 // 128):
                        act.wait_ge(m1_done, c * (M1 // 128) + (m + 1))
                        nc.scalar.activation(m1[:, m, :], mlp_banks[m][:, :], ACT.Relu, bias=b1_s[:, m:m + 1]).then_inc(m1_relu, 1)
                        act.wait_ge(m1_relu, c * (M1 // 128) + (m + 1))
                        nc.scalar.activation(m1_high[:, m, :], m1[:, m, :], ACT.Copy).then_inc(m1_rounded, 1)
                    for m in range(M2 // 128):
                        act.wait_ge(m2_done, c * (M2 // 128) + (m + 1))
                        nc.scalar.activation(m2[:, m, :], mlp_banks[4 + m][:, :], ACT.Relu, bias=b2_s[:, m:m + 1]).then_inc(m2_relu, 1)
                    act.wait_ge(y_done, c + 1)
                    nc.scalar.activation(ys[:, bass.ds(c * MLP_COLS, MLP_COLS)], cur1[0:1, :], ACT.Copy).then_inc(y_taken, 1)

            @block.vector
            def _(dve):
                def product(group, u, z, bank, chunk, other_in):
                    kind, _, ways = group
                    rows, n = rows_of(group), len(ways) - ways.count("d")
                    dve.wait_ge(spreads_made, u + 1)
                    dve.wait_ge(*other_in)
                    if n:
                        one = spread[bank][0:rows, :].unsqueeze(1).to_broadcast([rows, n, CHUNK])
                        other = aa[0:rows, 0:n, :] if kind == "B" else vv[0:rows, chunk % 2, 0:n, :]
                        nc.vector.tensor_tensor(zz[0:rows, z, 0:n, :], one, other, ALU.mult).then_inc(zz_made, 1)

                def product_d(group, bank, chunk, reads):
                    kind, _, ways = group
                    rows, n = rows_of(group), len(ways) - ways.count("d")
                    if "d" in ways:
                        if n:
                            dve.wait_ge(zz_made, reads)
                        other = aa[0:rows, n, :] if kind == "B" else vv[0:rows, chunk % 2, n, :]
                        nc.vector.tensor_tensor(spread[bank][0:rows, :], spread[bank][0:rows, :], other, ALU.mult).then_inc(d_made, 1)

                def rest_of(group, number, d, bank):
                    rows = rows_of(group)
                    if "d" in group[2]:
                        dve.wait_ge(high_d, number + 1)
                        nc.vector.tensor_tensor(dl[0:rows, d, :], spread[bank][0:rows, :], dh[0:rows, d, :].bitcast(f32),
                                                ALU.subtract).then_inc(low_d, 1)

                def split_rest(t, n):
                    dve.wait_ge(high_split, t * 2 + (n + 1))
                    if n == 0:
                        nc.vector.tensor_tensor(by_field(rest), by_field(emb), part(0), ALU.subtract).then_inc(low_split, 1)
                    else:
                        nc.vector.tensor_tensor(part(2), by_field(rest), part(1), ALU.subtract).then_inc(low_split, 1)

                def add_up(sums, cur, rows, first, free, made):
                    if first:
                        if free is not None:
                            dve.wait_ge(folds_made, free)
                        nc.vector.tensor_scalar(sums[0:rows, :], cur[0:rows, :], 0.0, None, ALU.max).then_inc(made, 1)
                    else:
                        nc.vector.scalar_tensor_tensor(out=sums[0:rows, :], in0=cur[0:rows, :], scalar=0.0, in1=sums[0:rows, :],
                                                       op0=ALU.max, op1=ALU.add).then_inc(made, 1)

                def fold(t, sums, feat, rows, made, ready, done):
                    dve.wait_ge(made, ready)
                    dve.wait_ge(folds_made, done - 2)
                    nc.vector.tensor_tensor(half[0:rows, :], sums[0:rows, 0:CHUNK // 2], sums[0:rows, CHUNK // 2:CHUNK],
                                            ALU.add).then_inc(folds_made, 1)
                    dve.wait_ge(folds_made, done - 1)
                    nc.vector.tensor_tensor(feat[0:rows, bass.ds(t * TILE, TILE)], half[0:rows, 0:TILE],
                                            half[0:rows, TILE:2 * TILE], ALU.add).then_inc(folds_made, 1)

                def fold0(t):
                    fold(t, sum0, feat0, H, sums0_made, t * 4 + 4, t * 4 + 3)

                def fold1(t):
                    fold(t, sum1, feat1, L, sums1_made, t * 4 + 5, t * 4 + 5)

                def slot_product(i, q, j, groups):
                    free = count_at(i, q, j) - (ZRING - 1)
                    if not isinstance(free, int) or free > 0:
                        dve.wait_ge(groups_done, free)
                    if groups[j][0] == "B":
                        other_in = aa_laid, i * (Q * AA) + (q + 2) * AA
                    else:
                        other_in = h_laid, i * (Q * V1 * 16) + (q + 1) * (V1 * 16)
                    product(groups[j], count_at(i, q, j), z_of(i, q, j), bank_of(i, q, j), q, other_in)

                def slot_product_d(i, q, j, groups):
                    product_d(groups[j], bank_of(i, q, j), q, count_at(i, q, j, "z", groups) + 1)

                def slot_rest(i, q, j, groups):
                    rest_of(groups[j], count_at(i, q, j, "d", groups), d_of(i, q, j, groups), bank_of(i, q, j))

                def slot(i, q, first=False, last=False):
                    groups = groups_of(q, last)
                    before = (i, q, AHEAD - 1, groups)
                    for n, at in enumerate(run_ahead(i, q, last)):
                        slot_product(*at)
                        slot_rest(*before)
                        slot_product_d(*at)
                        before = at
                        if q == Q - 1 and n == 0:
                            fold0(i)
                        if q == 0 and n + AHEAD == SUM1_AFTER + 1 and not first:
                            fold1(i - 1)
                        for part_no in range(2):
                            if q == 1 and not last and n + AHEAD == SPLIT[part_no][0]:
                                split_rest(i + 1, part_no)
                        if n + AHEAD == SUM0_AFTER and groups is GROUPS:
                            dve.wait_ge(groups_done, count_at(i, q, B0))
                            add_up(sum0, cur0, H, q == Q - 1, i * 4 + 3, sums0_made)
                        if n + AHEAD == (SUM1_AFTER if groups is GROUPS else AHEAD) and not first:
                            finish(i if q else i - 1, (q - 1) % Q, GROUPS)
                    if groups is LAST_GROUPS:
                        slot_rest(*before)
                        finish(i, q, groups)

                def finish(i, q, groups):
                    dve.wait_ge(groups_done, count_at(i, q, len(groups)))
                    add_up(sum1, cur0 if groups is LAST_GROUPS else cur1, L, q == 0, i * 4 + 1, sums1_made)

                dve.wait_ge(consts_in, 16 * CONSTS)
                nc.vector.tensor_tensor(w0[:, :, :], w0[:, :, :], w0t, ALU.add).then_inc(weights_ready, 1)
                dve.wait_ge(w0_high, 1)
                nc.vector.tensor_tensor(w0l[:, :, :], w0[:, :, :], w0h[:, :, :].bitcast(f32), ALU.subtract).then_inc(w0_split, 1)
                dve.wait_ge(w1_high, 1)
                nc.vector.tensor_tensor(w1l[:, :, :, :], w1s[:, :, :, :], w1h[:, :, :, :].bitcast(f32), ALU.subtract).then_inc(w1_split, 1)
                dve.wait_ge(wt_high, 1)
                nc.vector.tensor_tensor(wtl[:, :], wt, wth[:, :].bitcast(f32), ALU.subtract).then_inc(wt_split, 1)
                split_rest(0, 0)
                split_rest(0, 1)
                for b in range(B0):
                    product(GROUPS[b], b, b, b, 0, (aa_laid, AA))
                    if b:
                        rest_of(GROUPS[b - 1], number(b - 1, "d"), number(b - 1, "d"), b - 1)
                    product_d(GROUPS[b], b, 0, number(b, "z") + 1)
                rest_of(GROUPS[B0 - 1], number(B0 - 1, "d"), number(B0 - 1, "d"), B0 - 1)
                dve.wait_ge(groups_done, B0)
                add_up(sum0, cur0, H, True, None, sums0_made)
                dve.sem_inc(sums1_made, 1)
                dve.sem_inc(folds_made, 1)
                for j in range(AHEAD):
                    slot_product(0, 0, j, GROUPS)
                    if j:
                        slot_rest(0, 0, j - 1, GROUPS)
                    slot_product_d(0, 0, j, GROUPS)
                slot(0, 0, first=True)
                with dve.Fori(0, TILES - 1) as i:
                    for q in range(1, Q):
                        slot(i, q)
                    slot(i + 1, 0)
                for q in range(1, Q):
                    slot(TILES - 1, q, last=True)

                fold1(TILES - 1)

                with dve.Fori(0, STEPS) as c:
                    for n, (feat, rows) in enumerate([(feat0, H + DENSE), (feat1, L)]):
                        at = bass.ds(c * (2 * MLP_COLS) + n * MLP_COLS, MLP_COLS)
                        dve.wait_ge(feat_rounded, c * 2 + (n + 1))
                        nc.vector.tensor_tensor(feat_low[0:rows, at], feat[:, bass.ds(c * MLP_COLS, MLP_COLS)],
                                                feat_high[0:rows, at].bitcast(f32), ALU.subtract).then_inc(feat_split, 1)
                with dve.Fori(0, STEPS) as c:
                    for m in range(M1 // 128):
                        dve.wait_ge(m1_rounded, c * (M1 // 128) + (m + 1))
                        nc.vector.tensor_tensor(m1_low[:, m, :], m1[:, m, :], m1_high[:, m, :].bitcast(f32),
                                                ALU.subtract).then_inc(m1_split, 1)

            @block.tensor
            def _(pe):
                def make_copy(kind, bank, chunk):
                    x = xs[:, chunk % Q, :]
                    if kind == "xs":
                        for d in range(DQ):
                            last = nc.tensor.transpose(as_bf16(copied[bank])[:, d * TILE:(d + 1) * TILE],
                                                       parts[:, (chunk % Q) * DQ + d, :], selx[:, SELI:SELI + 128])
                    else:
                        last = nc.tensor.matmul(copied[bank][0:ROWSA, :], selx[:, SELA:SELA + ROWSA], x,
                                                start=True, stop=True)
                    last.then_inc(copies_made, 1)

                def make_spread(group, bank, chunk):
                    kind, b, _ = group
                    at, rows = (SELB + b * ROWS0, ROWS0) if kind == "B" else (SELO + b * 128, 128)
                    nc.tensor.matmul(spread[bank][0:rows, :], selx[:, at:at + rows], xs[:, chunk % Q, :],
                                     start=True, stop=True).then_inc(spreads_made, 1)

                def contract(group, acc, z, p_at, d_at, z_before, p_before, d_before):
                    kind, b, ways = group
                    rows = rows_of(group)
                    first = group in (GROUPS[0], GROUPS[B0])
                    final = group in (GROUPS[B0 - 1], GROUPS[-1])
                    terms = []
                    for v in sorted(range(len(ways)), key=lambda v: ("fdp".index(ways[v]), v)):
                        if kind == "B":
                            k = PAIRS0.index((b, v))
                            w, wh, wl = w0[:, k, :], w0h[:, k, :], w0l[:, k, :]
                        else:
                            w, wh, wl = w1s[:, b, v, :], w1h[:, b, v, :], w1l[:, b, v, :]
                        if ways[v] == "f":
                            terms.append((w, zz[:, z, v, :], (zz_made, z_before + 1)))
                        else:
                            if ways[v] == "d":
                                high, low, ready = dh[:, d_at, :], dl[:, d_at, :], (low_d, d_before + 1)
                            else:
                                high, low, ready = ph[:, p_at, v, :], pl[:, p_at, v, :], (low_p, p_before + 1)
                            terms += [(wh, high, ready), (wl, high, None), (wh, low, None)]
                    for n, (w, x, ready) in enumerate(terms):
                        if ready:
                            pe.wait_ge(*ready)
                        last = nc.tensor.matmul(acc[:, :], w[0:rows, :], x[0:rows, :], start=first and n == 0,
                                                stop=final and n == len(terms) - 1)
                    last.then_inc(groups_done, 1)

                def slot_copy(i, q, k, kind):
                    c = copy_at(i, q, k)
                    pe.wait_ge(copies_taken, c - 1)
                    if kind == "xs" and q == 2:
                        pe.wait_ge(low_split, i * 2 + 4)
                    if kind == "a":
                        pe.wait_ge(copies_taken, copy_at(i, q, 0) + 1)
                    make_copy(kind, copy_at(0, q, k) % 2, q + 2)

                def slot_spread(i, q, j, groups, used):
                    if has(used[3][used[2]], "d"):
                        pe.wait_ge(low_d, count_at(used[0], used[1], used[2], "d", used[3]) + 1)
                    else:
                        pe.wait_ge(zz_made, count_at(*used[:3], "z", used[3]) + 1)
                    make_spread(groups[j], bank_of(i, q, j), q + 1 if groups[j][0] == "B" else q)

                def slot(i, q, last=False):
                    groups = groups_of(q, last)
                    spreads = dict(enumerate(run_ahead(i, q, last)))
                    for j, group in enumerate(groups):
                        if j in spreads:
                            slot_spread(*spreads[j], (i, q, j, groups))
                        for k, (kind, before, _) in enumerate(copies_of(q, last)):
                            if before == j:
                                slot_copy(i, q, k, kind)
                        if j == 0:
                            pe.wait_ge(h_made, i * Q + (q + 1))
                            pe.wait_ge(sums0_made, i * Q + (q + 1))
                        if group == GROUPS[B0] and groups is GROUPS:
                            pe.wait_ge(sums1_made, i * Q + (q + 1))
                        contract(group, cur0 if group[0] == "B" or groups is LAST_GROUPS else cur1,
                                 z_of(i, q, j), p_of(i, q, j, groups), d_of(i, q, j, groups),
                                 count_at(i, q, j, "z", groups), count_at(i, q, j, "p", groups), count_at(i, q, j, "d", groups))

                pe.wait_ge(weights_ready, 1)
                pe.wait_ge(consts_in, 16 * CONSTS)
                pe.wait_ge(low_split, 2)
                make_copy("xs", 0, 0)
                pe.wait_ge(copies_taken, 1)
                make_copy("a", 1, 0)
                make_copy("xs", 0, 1)
                for b in range(B0):
                    make_spread(GROUPS[b], b, 0)
                pe.wait_ge(copies_taken, 3)
                make_copy("a", 1, 1)
                pe.wait_ge(w0_split, 1)
                for b in range(B0):
                    contract(GROUPS[b], cur0, b, number(b, "p"), number(b, "d"), number(b, "z"), number(b, "p"), number(b, "d"))
                pe.wait_ge(zz_made, number(B0, "z"))
                pe.wait_ge(low_d, number(B0, "d"))
                for j in range(AHEAD):
                    make_spread(GROUPS[j], bank_of(0, 0, j), 1 if j < B0 else 0)
                pe.wait_ge(w1_split, 1)
                slot(0, 0)
                with pe.Fori(0, TILES - 1) as i:
                    for q in range(1, Q):
                        slot(i, q)
                    slot(i + 1, 0)
                for q in range(1, Q):
                    slot(TILES - 1, q, last=True)

                def three_passes(bank, w, wrows, high, low, start, stop):
                    for n, (wx, x) in enumerate([(wth, high), (wtl, high), (wth, low)]):
                        last = nc.tensor.matmul(bank[:, :], wx[0:wrows, w:w + 128], x, start=start and n == 0, stop=stop and n == 2)
                    return last

                pe.wait_ge(mlp_in, 16 * MLPS)
                pe.wait_ge(wt_split, 1)
                pe.wait_ge(sums1_made, Q * TILES)
                pe.wait_ge(copies_taken, copy_at(TILES - 1, Q - 2, 0))
                with pe.Fori(0, STEPS) as c:
                    for m in range(M1 // 128):
                        for n, rows in enumerate([H + DENSE, L]):
                            if m == 0:
                                pe.wait_ge(feat_split, c * 2 + (n + 1))
                            at = bass.ds(c * (2 * MLP_COLS) + n * MLP_COLS, MLP_COLS)
                            last = three_passes(mlp_banks[m], n * M1 + m * 128, rows, feat_high[0:rows, at], feat_low[0:rows, at],
                                                n == 0, n == 1)
                        last.then_inc(m1_done, 1)
                    for k in range(M1 // 128):
                        pe.wait_ge(m1_split, c * (M1 // 128) + (k + 1))
                        for m in range(M2 // 128):
                            last = three_passes(mlp_banks[4 + m], 2 * M1 + k * M2 + m * 128, 128, m1_high[:, k, :], m1_low[:, k, :],
                                                k == 0, k == M1 // 128 - 1)
                            if k == M1 // 128 - 1:
                                last.then_inc(m2_done, 1)
                    pe.wait_ge(y_taken, c + 1)
                    for k in range(M2 // 128):
                        pe.wait_ge(m2_relu, c * (M2 // 128) + (k + 1))
                        last = nc.tensor.matmul(cur1[0:1, :], wt3_s[:, k:k + 1], m2[:, k, :], start=k == 0, stop=k == M2 // 128 - 1)
                    last.then_inc(y_done, 1)


def _indices():
    w0a = np.full((ROWS0, N0), -1)
    w0b = np.full((ROWS0, N0), -1)
    for p, (b, v) in enumerate(PAIRS0):
        for m in range(ROWS0):
            r, i = divmod(m, F)
            if R0 * (V0 * b + v) + r > F // 2:
                continue
            x, y = (i - R0 * v) % F, (i + R0 * V0 * b + r) % F
            w0a[m, p] = x * F + y
            if x != y:
                w0b[m, p] = y * F + x
    w1 = np.full((128, T1 * V1), -1)
    for t in range(T1):
        for v in range(V1):
            for m in range(A1 * J1):
                j, a = divmod(m, A1)
                if T1 * a + t < F:
                    w1[m, t * V1 + v] = (T1 * a + t) * H + J1 * v + j
    return w0a, w0b, w1


def _selections():
    x = np.zeros((128, ROWSA + B0 * ROWS0 + T1 * 128 + 128), np.float32)
    at = 0
    for m in range(ROWSA):
        for p in range(3):
            x[part_row(p, (m - R0 * (V0 - 1)) % F), at + m] = 1
    at += ROWSA
    for b in range(B0):
        for m in range(ROWS0):
            for p in range(3):
                x[part_row(p, (m % F + R0 * V0 * b + m // F) % F), at + m] = 1
        at += ROWS0
    for t in range(T1):
        for m in range(A1 * J1):
            for p in range(3):
                if T1 * (m % A1) + t < F:
                    x[part_row(p, T1 * (m % A1) + t), at + m] = 1
        at += 128
    x[:, at:] = np.eye(128)
    return x


def kernel(**inputs):
    import ml_dtypes
    import concourse.bacc as _bacc
    from concourse.bass_utils import run_bass_kernel_spmd as _run

    get = lambda n: np.asarray(inputs[n])

    def rows(w, at):
        out = w[np.maximum(at, 0)]
        out[at < 0] = 0
        return np.ascontiguousarray(out)

    w0a, w0b, w1 = _indices()
    sel_x = _selections()
    wt1 = get("W_top1")
    wl0 = np.concatenate([get("L0_rec_W0")[:, H:], get("L0_rec_W0")[:, :H]], axis=1)
    wt1a = np.concatenate([wt1[:L - H], wt1[L - H + L:], np.zeros((128 - H - DENSE, M1), wt1.dtype)], axis=0)
    wt2 = get("W_top2").reshape(M1 // 128, 128, M2).transpose(1, 0, 2).reshape(128, -1)
    wts = np.concatenate([wt1a, wt1[L - H:L - H + L], wt2], axis=1)
    arrays = {
        "ids": np.concatenate([get("ids"), np.zeros((2 * TILE, F), get("ids").dtype)], axis=0),
        **{f"tbl_{f}": get(f"tbl_{f}") for f in range(F)},
        "sel_x": sel_x.astype(ml_dtypes.bfloat16),
        "w0a": rows(wl0, w0a), "w0b": rows(wl0, w0b), "w1": rows(get("L0_rec_W1"), w1).reshape(128, T1, V1, L),
        "dense_t": np.ascontiguousarray(get("dense_ctx").T),
        "wts": wts,
        "wt3": get("W_top3").reshape(M2 // 128, 128).T,
        "b1": get("b_top1").reshape(M1 // 128, 128).T, "b2": get("b_top2").reshape(M2 // 128, 128).T,
    }
    arrays = {n: np.ascontiguousarray(a) for n, a in arrays.items()}
    nc = _bacc.Bacc("TRN2", target_bir_lowering=False, num_devices=1)
    d = {n: nc.dram_tensor(f"in_{n}", a.shape, mybir.dt.from_np(a.dtype), kind="ExternalInput").ap() for n, a in arrays.items()}
    out = nc.dram_tensor("out_y", (B, 1), mybir.dt.float32, kind="ExternalOutput").ap()
    build(nc, d["ids"], [d[f"tbl_{f}"] for f in range(F)], d["sel_x"], d["w0a"], d["w0b"], d["w1"], d["dense_t"],
          d["wts"], d["wt3"], d["b1"], d["b2"], out.rearrange("b one -> one b"))
    r = _run(nc, [{f"in_{n}": a for n, a in arrays.items()}], core_ids=[0])
    return r.results[0]["out_y"]
```
